# Optimizing a Trainium2 kernel written in Bass

```python
import numpy as np
import jax
import jax.numpy as jnp

def _softmax(x, axis=-1):
    return jax.nn.softmax(x, axis=axis)

def _gelu(x):
    return jax.nn.gelu(x, approximate=True)

def _silu(x):
    return jax.nn.silu(x)

def _sigmoid(x):
    return jax.nn.sigmoid(x)

def _layernorm(x, axis=-1, eps=1e-05):
    m = jnp.mean(x, axis=axis, keepdims=True)
    v = jnp.var(x, axis=axis, keepdims=True)
    return (x - m) / jnp.sqrt(v + eps)

def _scatter_add(tgt, idx, src, axis=0):
    return tgt.at[idx].add(src)

def _segment_sum(src, seg, n):
    return jax.ops.segment_sum(src, seg, n)
kernel_name = 'mk_adaln_attn_ffn_d1_seqx_r8_c066ac'

def setup_inputs(seed: int=0):
    np.random.seed(seed)
    _w = jnp.asarray

    def _rec_inputs():
        import jax
        import jax.numpy as jnp
        _rk = jax.random.key(seed)
        x = -0.000125 + 0.9999 * jax.random.normal(jax.random.fold_in(_rk, 1), (32, 32, 256), jnp.float32)
        _lenS = 32 - jax.random.randint(jax.random.fold_in(_rk, 7), (32,), 0, max(1, 32 // 4) + 1, jnp.int32)
        _lenS2 = 32 - jax.random.randint(jax.random.fold_in(_rk, 8), (32,), 0, max(1, 32 // 4) + 1, jnp.int32)
        itok_B_0_7 = jax.random.randint(jax.random.fold_in(_rk, 11), (32,), 0, 8, jnp.int32)
        fside_8xS_0 = -0.00162727 + 0.0609077 * jax.random.normal(jax.random.fold_in(_rk, 12), (8, 32), jnp.float32)
        return (x, itok_B_0_7, fside_8xS_0)
    x, itok_B_0_7, fside_8xS_0 = _rec_inputs()

    def _L0_cond_setup():
        import jax, jax.numpy as jnp
        import numpy as np
        B, C, T = (64, 32, 256)
        D, N = (32, 8)
        key = jax.random.key(seed)
        k_x, k_s, k_w, k_b = jax.random.split(key, 4)
        scale = 1.0 / np.sqrt(C)
        x = jax.random.normal(k_x, (B, C, T), dtype=jnp.float32)
        subjects = jax.random.randint(k_s, (B,), 0, N, dtype=jnp.int64)
        weights = jax.random.normal(k_w, (N, C, D), dtype=jnp.float32) * scale
        bias = jax.random.normal(k_b, (N, D), dtype=jnp.float32) * scale
        return {'x': x, 'subjects': subjects, 'weights': weights, 'bias': bias}
    _L0_cond_all = _L0_cond_setup()
    _L0_cond_in = {k: v for k, v in _L0_cond_all.items() if k in ('weights',)}
    del _L0_cond_all

    def _L0_attn_setup():
        import jax, jax.numpy as jnp
        import numpy as np
        N_HEADS = 16
        D_MODEL = 256
        D_HEAD = D_MODEL // N_HEADS
        B, T = (4, 256)
        key = jax.random.key(seed)
        k1, k2, k3 = jax.random.split(key, 3)
        x = jax.random.normal(k1, (B, T, D_MODEL), dtype=jnp.float32)
        W_qkv = jax.random.normal(k2, (D_MODEL, 3 * D_MODEL), dtype=jnp.float32) * D_MODEL ** (-0.5)
        b_qkv = jnp.zeros((3 * D_MODEL,), dtype=jnp.float32)
        W_out = jax.random.normal(k3, (D_MODEL, D_MODEL), dtype=jnp.float32) * D_MODEL ** (-0.5)
        b_out = jnp.zeros((D_MODEL,), dtype=jnp.float32)
        return {'x': x, 'W_qkv': W_qkv, 'b_qkv': b_qkv, 'W_out': W_out, 'b_out': b_out}
    _L0_attn_all = _L0_attn_setup()
    _L0_attn_in = {k: v for k, v in _L0_attn_all.items() if k in ('W_qkv', 'b_qkv', 'W_out', 'b_out')}
    del _L0_attn_all

    def _L0_cond2_setup():
        import jax, jax.numpy as jnp
        import numpy as np

        def _lora_linear(x, W, A, B, adapter_indices):
            base = jnp.einsum('bsd,df->bsf', x, W)
            Ai = A[adapter_indices]
            Bi = B[adapter_indices]
            lora = jnp.einsum('bsr,brf->bsf', jnp.einsum('bsd,bdr->bsr', x, Ai), Bi)
            return base + lora
        key = jax.random.key(seed)
        ks = jax.random.split(key, 10)
        H, I, N, R = (256, 1024, 8, 16)
        B, S = (4, 256)
        std_h = 1.0 / np.sqrt(H)
        std_i = 1.0 / np.sqrt(I)
        x = jax.random.normal(ks[0], (B, S, H), dtype=jnp.float32)
        adapter_indices = jax.random.randint(ks[1], (B,), 0, N, dtype=jnp.int32)
        Wg = jax.random.normal(ks[2], (H, I), dtype=jnp.float32) * std_h
        Wu = jax.random.normal(ks[3], (H, I), dtype=jnp.float32) * std_h
        Wd = jax.random.normal(ks[4], (I, H), dtype=jnp.float32) * std_i
        Ag = jax.random.normal(ks[5], (N, H, R), dtype=jnp.float32) * std_h
        Bg = jnp.zeros((N, R, I), dtype=jnp.float32) + 0.01
        Au = jax.random.normal(ks[6], (N, H, R), dtype=jnp.float32) * std_h
        Bu = jnp.zeros((N, R, I), dtype=jnp.float32) + 0.01
        Ad = jax.random.normal(ks[7], (N, I, R), dtype=jnp.float32) * std_i
        Bd = jnp.zeros((N, R, H), dtype=jnp.float32) + 0.01
        return {'x': x, 'Wg': Wg, 'Wu': Wu, 'Wd': Wd, 'Ag': Ag, 'Bg': Bg, 'Au': Au, 'Bu': Bu, 'Ad': Ad, 'Bd': Bd, 'adapter_indices': adapter_indices}
    _L0_cond2_all = _L0_cond2_setup()
    _L0_cond2_in = {k: v for k, v in _L0_cond2_all.items() if k in ('Wg', 'Wu', 'Wd', 'Ag', 'Bg', 'Au', 'Bu', 'Ad', 'Bd')}
    del _L0_cond2_all

    def _L0_ffn_setup():
        import jax, jax.numpy as jnp
        import numpy as np
        B, S, D, H = (4, 256, 256, 1024)

        def fwht(x):
            orig_shape = x.shape
            n = orig_shape[-1]
            x = x.reshape(-1, n)
            h = 1
            while h < n:
                xb = x.reshape(-1, n // (2 * h), 2, h)
                a = xb[:, :, 0, :]
                b = xb[:, :, 1, :]
                x = jnp.stack([a + b, a - b], axis=2).reshape(-1, n)
                h *= 2
            scale = jnp.asarray(1.0 / np.sqrt(n), dtype=x.dtype)
            return (x * scale).reshape(orig_shape)
        key = jax.random.key(seed)
        kx, k1, k2, k3 = jax.random.split(key, 4)
        x = jax.random.normal(kx, (B, S, D), dtype=jnp.float32)
        W1 = jax.random.normal(k1, (H, D), dtype=jnp.float32) * (1.0 / np.sqrt(D))
        W2 = jax.random.normal(k2, (D, H), dtype=jnp.float32) * (1.0 / np.sqrt(H))
        W3 = jax.random.normal(k3, (H, D), dtype=jnp.float32) * (1.0 / np.sqrt(D))
        return {'x': x, 'W1': W1, 'W2': W2, 'W3': W3}
    _L0_ffn_all = _L0_ffn_setup()
    _L0_ffn_in = {k: v for k, v in _L0_ffn_all.items() if k in ('W1', 'W2', 'W3')}
    del _L0_ffn_all
    return {'x': x, 'itok_B_0_7': itok_B_0_7, 'fside_8xS_0': fside_8xS_0, 'L0_cond_weights': _L0_cond_in['weights'], 'L0_attn_W_qkv': _L0_attn_in['W_qkv'], 'L0_attn_b_qkv': _L0_attn_in['b_qkv'], 'L0_attn_W_out': _L0_attn_in['W_out'], 'L0_attn_b_out': _L0_attn_in['b_out'], 'L0_cond2_Wg': _L0_cond2_in['Wg'], 'L0_cond2_Wu': _L0_cond2_in['Wu'], 'L0_cond2_Wd': _L0_cond2_in['Wd'], 'L0_cond2_Ag': _L0_cond2_in['Ag'], 'L0_cond2_Bg': _L0_cond2_in['Bg'], 'L0_cond2_Au': _L0_cond2_in['Au'], 'L0_cond2_Bu': _L0_cond2_in['Bu'], 'L0_cond2_Ad': _L0_cond2_in['Ad'], 'L0_cond2_Bd': _L0_cond2_in['Bd'], 'L0_ffn_W1': _L0_ffn_in['W1'], 'L0_ffn_W2': _L0_ffn_in['W2'], 'L0_ffn_W3': _L0_ffn_in['W3']}

def reference(x, itok_B_0_7, fside_8xS_0, L0_cond_weights, L0_attn_W_qkv, L0_attn_b_qkv, L0_attn_W_out, L0_attn_b_out, L0_cond2_Wg, L0_cond2_Wu, L0_cond2_Wd, L0_cond2_Ag, L0_cond2_Bg, L0_cond2_Au, L0_cond2_Bu, L0_cond2_Ad, L0_cond2_Bd, L0_ffn_W1, L0_ffn_W2, L0_ffn_W3):
    import jax
    import jax.numpy as jnp

    def _L0_cond_ref(x, subjects, weights, bias):
        import jax, jax.numpy as jnp
        import numpy as np
        B, C, T = (64, 32, 256)
        D, N = (32, 8)
        w = weights[subjects]
        b = bias[subjects]
        out = jnp.einsum('bct,bcd->bdt', x, w)
        out = out + b[:, :, None]
        return out

    def _L0_attn_ref(x, W_qkv, b_qkv, W_out, b_out):
        import jax, jax.numpy as jnp
        import numpy as np
        N_HEADS = 16
        D_MODEL = 256
        D_HEAD = D_MODEL // N_HEADS
        B, T = (4, 256)
        b, t, c = x.shape
        qkv = x @ W_qkv + b_qkv
        q, k, v = jnp.split(qkv, 3, axis=-1)

        def heads(u):
            return u.reshape(b, t, N_HEADS, D_HEAD).transpose(0, 2, 1, 3)
        q, k, v = (heads(q), heads(k), heads(v))
        scale = 1.0 / D_HEAD
        att = jnp.einsum('bhqd,bhkd->bhqk', q, k) * scale
        causal = jnp.tril(jnp.ones((t, t), dtype=bool))
        att = jnp.where(causal, att, -jnp.inf)
        att = jax.nn.softmax(att, axis=-1)
        y = jnp.einsum('bhqk,bhkd->bhqd', att, v)
        y = y.transpose(0, 2, 1, 3).reshape(b, t, c)
        return y @ W_out + b_out

    def _L0_cond2_ref(x, Wg, Wu, Wd, Ag, Bg, Au, Bu, Ad, Bd, adapter_indices):
        import jax, jax.numpy as jnp
        import numpy as np

        def _lora_linear(x, W, A, B, adapter_indices):
            base = jnp.einsum('bsd,df->bsf', x, W)
            Ai = A[adapter_indices]
            Bi = B[adapter_indices]
            lora = jnp.einsum('bsr,brf->bsf', jnp.einsum('bsd,bdr->bsr', x, Ai), Bi)
            return base + lora
        gate = _lora_linear(x, Wg, Ag, Bg, adapter_indices)
        up = _lora_linear(x, Wu, Au, Bu, adapter_indices)
        h = jax.nn.silu(gate) * up
        return _lora_linear(h, Wd, Ad, Bd, adapter_indices)

    def _L0_ffn_ref(x, W1, W2, W3):
        import jax, jax.numpy as jnp
        import numpy as np
        B, S, D, H = (4, 256, 256, 1024)

        def fwht(x):
            orig_shape = x.shape
            n = orig_shape[-1]
            x = x.reshape(-1, n)
            h = 1
            while h < n:
                xb = x.reshape(-1, n // (2 * h), 2, h)
                a = xb[:, :, 0, :]
                b = xb[:, :, 1, :]
                x = jnp.stack([a + b, a - b], axis=2).reshape(-1, n)
                h *= 2
            scale = jnp.asarray(1.0 / np.sqrt(n), dtype=x.dtype)
            return (x * scale).reshape(orig_shape)
        up_gate = jnp.einsum('bsd,hd->bsh', x, W1)
        up_lin = jnp.einsum('bsd,hd->bsh', x, W3)
        hidden = jax.nn.silu(up_gate) * up_lin
        hidden = fwht(hidden)
        out = jnp.einsum('bsh,dh->bsd', hidden, W2)
        return out
    x = x + _L0_attn_ref(_L0_cond_ref(x, itok_B_0_7, L0_cond_weights, fside_8xS_0), L0_attn_W_qkv, L0_attn_b_qkv, L0_attn_W_out, L0_attn_b_out)
    x = x + _L0_ffn_ref(_L0_cond2_ref(x, L0_cond2_Wg, L0_cond2_Wu, L0_cond2_Wd, L0_cond2_Ag, L0_cond2_Bg, L0_cond2_Au, L0_cond2_Bu, L0_cond2_Ad, L0_cond2_Bd, itok_B_0_7), L0_ffn_W1, L0_ffn_W2, L0_ffn_W3)
    return x

_drawn_inputs = setup_inputs


def setup_inputs(seed=0):
    import zlib

    import numpy as np

    out = dict(_drawn_inputs(seed))
    spreads = {'L0_attn_b_qkv': (0.0, 0.1),
     'L0_attn_b_out': (0.0, 0.1),
     'L0_cond2_Bg': (0.009999999776482582, 0.6),
     'L0_cond2_Bu': (0.009999999776482582, 0.6),
     'L0_cond2_Bd': (0.009999999776482582, 0.6)}
    factors = {'L0_cond2_Au': 2.83, 'L0_cond2_Ad': 3.247}
    for name, (base, spread) in spreads.items():
        noise = np.random.default_rng([zlib.crc32(name.encode()), seed]).standard_normal(out[name].shape)
        drawn = base * np.exp(spread * noise) if base else spread * noise
        out[name] = jnp.asarray(drawn.astype(out[name].dtype))
    for name, factor in factors.items():
        out[name] = (out[name] * factor).astype(out[name].dtype)
    return out
```

```python
from contextlib import ExitStack

import numpy as np

import concourse.bass as bass
from concourse import mybir

F32 = mybir.dt.float32
F32R = mybir.dt.float32r
BF16 = mybir.dt.bfloat16
I32 = mybir.dt.int32
ALU = mybir.AluOpType
ACT = mybir.ActivationFunctionType
AX = mybir.AxisListType

P = 128
B, T, D = 32, 32, 256
TOK = B * T
HALVES = 2
HT = TOK // HALVES
BH = B // HALVES
SLOTS = P // T
GROUPS = BH // SLOTS
DC = D // P
NH, DH = 16, 16
PAIRS = P // (2 * DH)
N, R = 8, 16
H = 1024
HC = H // P
SCALE = 1.0 / DH
MASKED = -1e30

C_HAD, C_ONES, C_ID, C_CAUSAL = 0, P, 2 * P, 3 * P
C_NROW = C_CAUSAL + T
C_NCOL = C_NROW + N
C_PCOL = C_NCOL + 1
C_PAR = C_PCOL + 1
C_SLOT = C_PAR + 2
C_END = C_SLOT + SLOTS
B_Q, B_K, B_V, B_O = 0, DC, 2 * DC, 3 * DC

W_Q, W_K, W_V, W_OUT, W_A, W_GU = 0, 1, 2, 3, 4, 5
W_D0 = W_GU + HC
W_AD, W_D1, W_BD = W_D0 + 1, W_D0 + 2, W_D0 + 3
W_F = W_BD + 1
BATCHES = W_F + HC
COLS = ([DC * DC * P] * 5 + [(DC + 1) * 2 * P] * HC + [HC * P] * 3 + [DC * P] + [DC * 2 * P] * HC)
RING = 6144
STAGES = 3
STAGE_COLS = max(COLS)
STARTS = [sum(COLS[:i]) for i in range(BATCHES)]


def ring_places():
    places, live, at = [], [], 0
    for n, cols in enumerate(COLS):
        if at + cols > RING:
            at = 0
        need = max([m + 1 for m, lo, hi in live if lo < at + cols and at < hi], default=0)
        live = [(m, lo, hi) for m, lo, hi in live if m + 1 > need] + [(n, at, at + cols)]
        places.append((at, need))
        at += cols
    return places


PLACES = ring_places()


def psum_tiles():
    names = [("xc", s, c) for s in range(HALVES) for c in range(DC)]

    def qkv(s):
        return [("q", s, m) for m in range(DC)] + [("k", s, m) for m in range(DC)] + [
            ("v", s, j) for j in range(GROUPS // 2)]

    names += qkv(0) + [("fold", 0, j) for j in range(4)] + [("s", 0, i) for i in range(PAIRS)]
    names += qkv(1) + [("s", 1, i) for i in range(PAIRS)]
    names += [("y", s, i) for s in range(HALVES) for i in range(SLOTS)]
    names += [("o", s, m) for s in range(HALVES) for m in range(DC)]
    names += [("z", s, a) for s in range(HALVES) for a in range(2)]
    names += [(a, s, m) for m in range(HC) for a in ("gate", "up") for s in range(HALVES)]
    names += [(a, s, 0) for a in ("d0", "zd", "d1") for s in range(HALVES)]
    names += [(a, s, m) for m in range(HC) for a in ("f1", "f3") for s in range(HALVES)]
    names += [("w2", s, m) for m in range(DC) for s in range(HALVES)]
    return {name: (n % 8, n // 8) for n, name in enumerate(names)}


TILES = psum_tiles()
LAST_USE = ([("q", 1, 1), ("k", 1, 1), ("v", 1, 1), ("o", 1, 1), ("z", 1, 1)]
            + [("up", 1, m) for m in range(HC)] + [("zd", 1, 0)] * 2 + [("d1", 1, 0)] * 2
            + [("f3", 1, m) for m in range(HC)])
GATED = [(name, s, m) for name in ("up", "f3") for m in range(HC) for s in range(HALVES)]
PRODUCTS = ([("z", s, a) for s in range(HALVES) for a in range(2)] + GATED[:2 * HC]
            + [("zd", s, 0) for s in range(HALVES)] + GATED[2 * HC:])


def build(nc, x_slots, x_feat, index, index_slots, fside, cond_w, biases, w_stream, w2_t, consts, out):
    with ExitStack() as ctx:
        def sb(name, shape, dt=F32):
            return ctx.enter_context(nc.sbuf_tensor(name, shape, dt))

        def sem(name):
            return ctx.enter_context(nc.semaphore(name))

        const = sb("const", [P, C_END])
        bias = sb("bias", [P, 4 * DC])
        idx_slot_i = sb("idx_slot_i", [P, HALVES * GROUPS], I32)
        idx_row_i = sb("idx_row_i", [P, B], I32)
        idx_slot = sb("idx_slot", [P, HALVES * GROUPS])
        idx_row = sb("idx_row", [P, B])
        onehot_slot = sb("onehot_slot", [P, HALVES * GROUPS, N])
        onehot_n = sb("onehot_n", [P, B])
        adapter_mask = sb("adapter_mask", [P, B])
        fs = sb("fs", [N, T])
        k_bias = sb("k_bias", [P, DC, 2])
        ident_bf = sb("ident_bf", [P, P], BF16)
        causal_bf = sb("causal_bf", [P, 2 * PAIRS * 2, T], BF16)
        row_max = sb("row_max", [P, HALVES, PAIRS, 16])
        row_sum = sb("row_sum", [P, HALVES, PAIRS, 16])
        row_inv = sb("row_inv", [P, HALVES, PAIRS, 16])
        resid = sb("resid", [P, DC, TOK])
        raw = sb("raw", [P, STAGES, STAGE_COLS])
        tmp_a = sb("tmp_a", [P, 4, HT])
        tmp_b = sb("tmp_b", [P, 4, HT])
        w_hi = sb("w_hi", [P, RING], F32R)
        w_lo = sb("w_lo", [P, RING], F32R)
        w2_hi = sb("w2_hi", [P, HC, D], F32R)
        w2_lo = sb("w2_lo", [P, HC, D], F32R)
        act_hi = sb("act_hi", [P, DC, TOK], F32R)
        act_lo = sb("act_lo", [P, DC, TOK], F32R)
        aux_hi = sb("aux_hi", [P, DC, TOK], F32R)
        aux_lo = sb("aux_lo", [P, DC, TOK], F32R)
        with ExitStack() as early:
            def eb(name, shape, dt=F32):
                return early.enter_context(nc.sbuf_tensor(name, shape, dt))
            q_t = eb("q_t", [P, DC, TOK])
            k_x = eb("k_x", [P, DC, B, 2, T])
            v_tok = eb("v_tok", [P, HALVES * GROUPS, D])
            prob = eb("prob", [P, HALVES, PAIRS, 16, T])
            prob_t = eb("prob_t", [P, HALVES, PAIRS, 16, T])
        h_hi = sb("h_hi", [P, HC, TOK], F32R)
        h_lo = sb("h_lo", [P, HC, TOK], F32R)
        flat_t = prob_t[:, :, :, :, :].rearrange("p s i r k -> p (s i r k)")
        x_slot = flat_t[:, 0:2048].rearrange("p (g d) -> p g d", d=D)
        cond_prod = flat_t[:, 2048:4096].rearrange("p (g d n) -> p g d n", d=T, n=N)
        flat_p = prob[:, :, :, :, :].rearrange("p s i r k -> p (s i r k)")
        cond_sel = flat_p[:, 2048:2304].rearrange("p (g d) -> p g d", d=T)
        cond_blk = flat_p[:, 2304:3328].rearrange("p (g j d) -> p g j d", j=SLOTS, d=T)
        cond_all = flat_p[:, 3328:3584].rearrange("p (d n) -> p d n", n=N)
        fbias = q_t[:, 0, :].rearrange("p (b d) -> p b d", d=T)
        had = const[:, C_HAD:C_HAD + P]
        ones = const[:, C_ONES:C_ONES + P]
        parity = const[:, C_PAR:C_PAR + 2]

        banks = [ctx.enter_context(nc.psum_tensor(f"bank{i}", [P, HT], F32)) for i in range(8)]

        small_loaded = sem("small_loaded")
        x_loaded = [sem(f"x_loaded{s}") for s in range(HALVES)]
        resid_loaded = sem("resid_loaded")
        w2_loaded = sem("w2_loaded")
        raw_loaded = [sem(f"raw_loaded{j}") for j in range(STAGES)]
        w_hi_made = sem("w_hi_made")
        w_lo_made = sem("w_lo_made")
        bank_full = [sem(f"bank_full{i}") for i in range(8)]
        bank_free = [sem(f"bank_free{i}") for i in range(8)]
        setup = sem("setup")
        ident_made = sem("ident_made")
        causal_made = sem("causal_made")
        fbias_made = sem("fbias_made")
        cond_made = sem("cond_made")
        xc_hi_made = sem("xc_hi_made")
        butterfly = sem("butterfly")
        w2_hi_made = sem("w2_hi_made")
        w2_split = sem("w2_split")
        max_made = sem("max_made")
        exp_made = sem("exp_made")
        sum_made = sem("sum_made")
        inv_made = sem("inv_made")
        normed = sem("normed")
        prob_t_made = sem("prob_t_made")
        y_even = sem("y_even")
        y_hi_made = sem("y_hi_made")
        y_split = sem("y_split")
        x1_hi_made = sem("x1_hi_made")
        x1_split = sem("x1_split")
        prod_hi_made = sem("prod_hi_made")
        prod_split = sem("prod_split")
        y2_hi_made = sem("y2_hi_made")
        out_made = sem("out_made")
        out_stored = sem("out_stored")

        SMALL = 4 + 2 * SLOTS

        Z, GU, ZD, FF = 0, 4, 4 + 2 * HC, 6 + 2 * HC
        LAST = FF + 2 * HC

        def tile(name, s, m):
            return banks[TILES[name, s, m][0]]

        def wait_full(eng, name, s, m):
            bank, before = TILES[name, s, m]
            eng.wait_ge(bank_full[bank], before + 1)

        def full(ins, name, s, m):
            ins.then_inc(bank_full[TILES[name, s, m][0]], 1)

        def free(ins, name, s, m):
            ins.then_inc(bank_free[TILES[name, s, m][0]], 1)

        def wait_read(eng, name, s, m):
            bank, before = TILES[name, s, m]
            eng.wait_ge(bank_free[bank], before + 1)

        def half(s):
            return slice(s * HT, (s + 1) * HT)

        def by_slot(s, j):
            return q_t[:, :, half(s)].rearrange("p c (g j t) -> p j c g t", g=GROUPS, j=SLOTS)[:, j]

        def f32(ap):
            return ap.bitcast(F32)

        block = ctx.enter_context(nc.Block())

        @block.sync
        def _(sp):
            for j in range(SLOTS):
                rows = slice(j * T, (j + 1) * T)
                src = index_slots[j:j + 1, :]
                sp.dma_start(idx_slot_i[rows, :], src.to_broadcast([T, HALVES * GROUPS])).then_inc(small_loaded, 16)
                sp.dma_start(cond_all[rows], cond_w).then_inc(small_loaded, 16)
            sp.dma_start(const[:, :], consts).then_inc(small_loaded, 16)
            sp.dma_start(idx_row_i[:, :], index.rearrange("(a n) -> a n", a=1).to_broadcast([P, B]))\
              .then_inc(small_loaded, 16)
            sp.dma_start(fs[:, :], fside).then_inc(small_loaded, 16)
            sp.dma_start(bias[:, :], biases).then_inc(small_loaded, 16)

            def load_weights(n):
                if n >= STAGES:
                    sp.wait_ge(w_lo_made, n - STAGES + 1)
                sp.dma_start(raw[:, n % STAGES, 0:COLS[n]], w_stream[:, STARTS[n]:STARTS[n] + COLS[n]])\
                  .then_inc(raw_loaded[n % STAGES], 16)

            for n in range(STAGES):
                load_weights(n)
            sp.dma_start(tmp_b[:, :, :], w2_t.rearrange("p (j n) -> p j n", j=4)).then_inc(w2_loaded, 16)
            sp.dma_start(resid[:, :, :], x_feat).then_inc(resid_loaded, 16)
            for n in range(STAGES, BATCHES):
                load_weights(n)
            for j in range(4):
                m, s = j // HALVES, j % HALVES
                sp.wait_ge(out_made, j + 1)
                sp.dma_start(out[m * P:(m + 1) * P, half(s)], tmp_b[:, (LAST + j) % 4, :])\
                  .then_inc(out_stored, 16)
            sp.wait_ge(out_stored, 4 * 16)

        @block.tensor
        def _(pe):
            def claim(name, s, m):
                bank, before = TILES[name, s, m]
                if before:
                    pe.wait_ge(bank_free[bank], before)
                return banks[bank]

            def weights(n):
                pe.wait_ge(w_lo_made, n + 1)
                at = PLACES[n][0]
                return w_hi[:, at:at + COLS[n]], w_lo[:, at:at + COLS[n]]

            def unit(w, u):
                return w[0][:, u * P:(u + 1) * P], w[1][:, u * P:(u + 1) * P]

            def both(tiles, w, xs, start, stop):
                last = []
                for ps, (x_hi, _) in zip(tiles, xs):
                    pe.matmul(ps[:, :], w[0], x_hi, start=start, stop=False)
                for ps, (_, x_lo) in zip(tiles, xs):
                    pe.matmul(ps[:, :], w[0], x_lo, start=False, stop=False)
                for ps, (x_hi, _) in zip(tiles, xs):
                    last.append(pe.matmul(ps[:, :], w[1], x_hi, start=False, stop=stop))
                return last

            def rows(hi, lo, c, ss=(0, 1)):
                return [(hi[:, c, half(s)], lo[:, c, half(s)]) for s in ss]

            pe.wait_ge(small_loaded, 16 * SMALL)
            for s in range(HALVES):
                for c in range(DC):
                    ps = claim("xc", s, c)
                    if c == 0:
                        pe.wait_ge(fbias_made, 1)
                    pe.matmul(ps[:, :], ones[0:N, :], fbias[0:N, s * BH:(s + 1) * BH, :],
                              start=True, stop=False, skip_group_check=True)
                    if c == 0:
                        pe.wait_ge(cond_made, 1)
                        pe.wait_ge(x_loaded[s], 16)
                    for g in range(GROUPS):
                        last = pe.matmul(ps[:, g * P:(g + 1) * P], x_slot[:, s * GROUPS + g, c * P:(c + 1) * P],
                                         cond_blk[:, s * GROUPS + g], start=False,
                                         stop=(g == GROUPS - 1), skip_group_check=True)
                    full(last, "xc", s, c)

            def qkv(s):
                for c in range(DC):
                    wait_read(pe, "xc", s, c)
                for name, n in (("q", W_Q), ("k", W_K)):
                    w = weights(n)
                    for m in range(DC):
                        ps = claim(name, s, m)
                        for c in range(DC):
                            last = both([ps], unit(w, m * DC + c), rows(act_hi, act_lo, c, [s]),
                                        c == 0, c == DC - 1)
                        full(last[0], name, s, m)
                w = weights(W_V)
                for j in range(GROUPS // 2):
                    ps = claim("v", s, j)
                    for g2 in range(2):
                        for c in range(DC):
                            at = s * HT + (2 * j + g2) * P
                            x_hi, x_lo = act_hi[:, c, at:at + P], act_lo[:, c, at:at + P]
                            wv = [a[:, c * D:(c + 1) * D] for a in w]
                            o = ps[:, g2 * D:(g2 + 1) * D]
                            pe.matmul(o, x_hi, wv[0], start=(c == 0), stop=False)
                            pe.matmul(o, x_hi, wv[1], start=False, stop=False)
                            last = pe.matmul(o, x_lo, wv[0], start=False, stop=(c == DC - 1))
                    full(last, "v", s, j)

            def scores(s):
                tiles = [claim("s", s, i) for i in range(PAIRS)]
                pe.wait_ge(ident_made, 1)
                pe.wait_ge(causal_made, 1)
                for ps in tiles:
                    pe.matmul(ps[:, :], ident_bf[:, :], causal_bf[:, :, :], start=True, stop=False,
                              skip_group_check=True)
                for c in range(DC):
                    wait_read(pe, "q", s, c)
                    wait_read(pe, "k", s, c)
                for g in range(GROUPS):
                    for c in range(DC):
                        for j in range(SLOTS):
                            b = s * BH + g * SLOTS + j
                            for i in range(PAIRS):
                                q = slice(32 * i, 32 * i + 32)
                                at = (g * DC + c) * 2 * T
                                end = g == GROUPS - 1 and c == DC - 1 and j == SLOTS - 1
                                last = pe.matmul(tiles[i][32 * j:32 * j + 32, at:at + 2 * T],
                                                 q_t[q, c, b * T:(b + 1) * T], k_x[q, c, b],
                                                 start=False, stop=end, skip_group_check=True)
                                if end:
                                    full(last, "s", s, i)

            def fold():
                pe.wait_ge(w2_loaded, 16)
                for j in range(4):
                    ps = claim("fold", 0, j)
                    full(pe.matmul(ps[:, :], had, tmp_b[:, j, :], start=True, stop=True), "fold", 0, j)

            def values(s):
                tiles = [claim("y", s, j) for j in range(SLOTS)]
                for j in range(GROUPS // 2):
                    wait_read(pe, "v", s, j)
                for i in range(PAIRS):
                    pe.wait_ge(prob_t_made, PAIRS * s + i + 1)
                    for g in range(GROUPS):
                        for c in range(DC):
                            for j in range(SLOTS):
                                rows_ = slice(32 * j, 32 * j + 32)
                                o = tiles[j][32 * i:32 * i + 32, :].rearrange(
                                    "p (h c g t) -> p c g h t", h=2, c=DC, g=GROUPS)[:, c, g]
                                end = i == PAIRS - 1 and g == GROUPS - 1 and c == DC - 1
                                r = (g * DC + c) * 2
                                last = pe.matmul(o, v_tok[rows_, s * GROUPS + g, c * P + 32 * i:c * P + 32 * i + 32],
                                                 prob_t[rows_, s, i, r:r + 2], start=True, stop=True,
                                                 skip_group_check=True)
                                if end:
                                    full(last, "y", s, j)

            def project(s):
                w = weights(W_OUT)
                for m in range(DC):
                    ps = claim("o", s, m)
                    pe.wait_ge(y_split, DC * (s + 1))
                    for c in range(DC):
                        last = both([ps], unit(w, m * DC + c), rows(aux_hi, aux_lo, c, [s]), c == 0, c == DC - 1)
                    full(last[0], "o", s, m)

            def adapters_in(s):
                w = weights(W_A)
                for a in range(2):
                    ps = claim("z", s, a)
                    pe.wait_ge(x1_split, DC * (s + 1))
                    for c in range(DC):
                        last = both([ps], unit(w, a * DC + c), rows(act_hi, act_lo, c, [s]), c == 0, c == DC - 1)
                    full(last[0], "z", s, a)

            qkv(0)
            fold()
            scores(0)
            qkv(1)
            scores(1)
            values(0)
            values(1)
            project(0)
            project(1)
            adapters_in(0)
            adapters_in(1)

            for m in range(HC):
                w = weights(W_GU + m)
                for a, name in enumerate(("gate", "up")):
                    tiles = [claim(name, s, m) for s in range(HALVES)]
                    for c in range(DC):
                        both(tiles, unit(w, a * (DC + 1) + c), rows(act_hi, act_lo, c), c == 0, False)
                    pe.wait_ge(prod_split, Z + 4)
                    last = both(tiles, unit(w, a * (DC + 1) + DC), rows(aux_hi, aux_lo, a), False, True)
                    for s in range(HALVES):
                        full(last[s], name, s, m)

            down = {}
            for name, n in (("d0", W_D0), ("zd", W_AD), ("d1", W_D1)):
                w = weights(n)
                tiles = down[name] = [claim(name, s, 0) for s in range(HALVES)]
                for k in range(HC):
                    pe.wait_ge(prod_split, GU + 2 * k + 2)
                    last = both(tiles, unit(w, k), rows(h_hi, h_lo, k), k == 0, name == "zd" and k == HC - 1)
                if name == "zd":
                    for s in range(HALVES):
                        full(last[s], name, s, 0)
            w = weights(W_BD)
            pe.wait_ge(prod_split, ZD + 2)
            for s in range(HALVES):
                for m, name in enumerate(("d0", "d1")):
                    last = both([down[name][s]], unit(w, m), rows(aux_hi, aux_lo, 0, [s]), False, True)
                    full(last[0], name, s, 0)

            for m in range(HC):
                w = weights(W_F + m)
                for a, name in enumerate(("f1", "f3")):
                    tiles = [claim(name, s, m) for s in range(HALVES)]
                    for s in range(HALVES):
                        wait_read(pe, "d0", s, 0)
                        wait_read(pe, "d1", s, 0)
                    for c in range(DC):
                        last = both(tiles, unit(w, a * DC + c), rows(act_hi, act_lo, c), c == 0, c == DC - 1)
                    for s in range(HALVES):
                        full(last[s], name, s, m)

            pe.wait_ge(w2_split, 4)
            for m in range(DC):
                tiles = [claim("w2", s, m) for s in range(HALVES)]
                if m == DC - 1:
                    steps = [[0], [1]]
                else:
                    steps = [[0, 1]]
                for ss in steps:
                    for k in range(HC):
                        pe.wait_ge(prod_split, FF + 2 * k + 2)
                        w = (w2_hi[:, k, m * P:(m + 1) * P], w2_lo[:, k, m * P:(m + 1) * P])
                        last = both([tiles[s] for s in ss], w, rows(h_hi, h_lo, k, ss), k == 0, k == HC - 1)
                    for s, ins in zip(ss, last):
                        full(ins, "w2", s, m)

        @block.scalar
        def _(act):
            for s in range(HALVES):
                act.dma_start(x_slot[:, s * GROUPS:(s + 1) * GROUPS, :],
                              x_slots[:, s * GROUPS:(s + 1) * GROUPS, :]).then_inc(x_loaded[s], 16)

            def split_weights(n):
                act.wait_ge(raw_loaded[n % STAGES], 16 * (n // STAGES + 1))
                at, need = PLACES[n]
                if need:
                    wait_full(act, *LAST_USE[need - 1])
                act.activation(w_hi[:, at:at + COLS[n]], raw[:, n % STAGES, 0:COLS[n]], ACT.Copy)\
                   .then_inc(w_hi_made, 1)

            split_weights(W_Q)
            split_weights(W_K)
            split_weights(W_V)
            for s in range(HALVES):
                for c in range(DC):
                    wait_full(act, "xc", s, c)
                    act.activation(act_hi[:, c, half(s)], tile("xc", s, c)[:, :], ACT.Copy)\
                       .then_inc(xc_hi_made, 1)

            def evacuate_qv(s):
                for m in range(DC):
                    wait_full(act, "q", s, m)
                    free(act.activation(q_t[:, m, half(s)], tile("q", s, m)[:, :], ACT.Identity,
                                        bias=bias[:, B_Q + m:B_Q + m + 1]), "q", s, m)
                for j in range(GROUPS // 2):
                    wait_full(act, "v", s, j)
                    g = s * GROUPS + 2 * j
                    free(act.activation(v_tok[:, g:g + 2, :], tile("v", s, j)[:, :].rearrange(
                        "p (g d) -> p g d", g=2), ACT.Copy), "v", s, j)

            def exps(s):
                for i in range(PAIRS):
                    wait_read(act, "s", s, i)
                    act.activation(prob[:, s, i], prob[:, s, i], ACT.Exp, scale=SCALE).then_inc(exp_made, 1)

            evacuate_qv(0)
            for j in range(4):
                wait_full(act, "fold", 0, j)
                free(act.activation(tmp_a[:, j, :], tile("fold", 0, j)[:, :], ACT.Copy), "fold", 0, j)
            split_weights(W_OUT)
            split_weights(W_A)
            exps(0)
            evacuate_qv(1)
            split_weights(W_GU)
            exps(1)
            split_weights(W_GU + 1)
            for j in range(4):
                act.wait_ge(butterfly, 6)
                part = w2_hi[:, 2 * j:2 * j + 2, :].rearrange("p k d -> p (k d)")
                act.activation(part, tmp_b[:, j, :], ACT.Copy).then_inc(w2_hi_made, 1)

            def attention_out(s):
                for j in range(SLOTS):
                    wait_full(act, "y", s, j)
                    ps = tile("y", s, j)[:, :].rearrange("p (h c g t) -> p h c g t", h=2, c=DC, g=GROUPS)
                    act.activation(by_slot(s, j), ps[:, 0], ACT.Copy, scale=parity[:, 0:1])\
                       .then_inc(y_even, 1)
                for c in range(DC):
                    for j in range(SLOTS):
                        wait_read(act, "y", s, j)
                    act.activation(aux_hi[:, c, half(s)], q_t[:, c, half(s)], ACT.Identity,
                                   bias=bias[:, B_V + c:B_V + c + 1]).then_inc(y_hi_made, 1)

            attention_out(0)
            attention_out(1)
            for s in range(HALVES):
                for m in range(DC):
                    wait_read(act, "o", s, m)
                    act.activation(act_hi[:, m, half(s)], resid[:, m, half(s)], ACT.Copy)\
                       .then_inc(x1_hi_made, 1)

            def product_hi(n, dst):
                wait_read(act, *PRODUCTS[n])
                act.activation(dst, tmp_b[:, n % 4, :], ACT.Copy).then_inc(prod_hi_made, 1)

            def silu(n, name, s, m):
                if n == 0:
                    act.wait_ge(butterfly, 6)
                if n >= 4:
                    wait_read(act, *GATED[n - 4])
                wait_full(act, name, s, m)
                free(act.activation(tmp_a[:, n % 4, :], tile(name, s, m)[:, :], ACT.Silu), name, s, m)

            for n in range(4):
                product_hi(Z + n, aux_hi[:, n % 2, half(n // 2)])
            split_weights(W_GU + 2)
            for m in range(HC):
                for s in range(HALVES):
                    silu(2 * m + s, "gate", s, m)
                split_weights(W_GU + m + 3)
                for s in range(HALVES):
                    product_hi(GU + 2 * m + s, h_hi[:, m, half(s)])
            for s in range(HALVES):
                product_hi(ZD + s, aux_hi[:, 0, half(s)])
            split_weights(W_GU + HC + 3)
            split_weights(W_F)
            for s in range(HALVES):
                for m, name in enumerate(("d0", "d1")):
                    wait_full(act, name, s, 0)
                    act.activation(act_hi[:, m, half(s)], tile(name, s, 0)[:, :], ACT.Copy)\
                       .then_inc(y2_hi_made, 1)
            for m in range(HC):
                if m + 1 < HC:
                    split_weights(W_F + m + 1)
                for s in range(HALVES):
                    silu(2 * HC + 2 * m + s, "f1", s, m)
                for s in range(HALVES):
                    product_hi(FF + 2 * m + s, h_hi[:, m, half(s)])

        @block.vector
        def _(dve):
            dve.wait_ge(small_loaded, 16 * SMALL)
            dve.tensor_copy(idx_slot[:, :], idx_slot_i[:, :]).then_inc(setup, 1)
            dve.tensor_copy(idx_row[:, :], idx_row_i[:, :]).then_inc(setup, 1)
            groups = HALVES * GROUPS
            dve.wait_ge(setup, 1)
            dve.tensor_tensor(onehot_slot[:, :, :], idx_slot[:, :].unsqueeze(2).to_broadcast([P, groups, N]),
                              const[:, C_NROW:C_NROW + N].unsqueeze(1).to_broadcast([P, groups, N]),
                              ALU.is_equal).then_inc(setup, 1)
            dve.wait_ge(setup, 2)
            dve.tensor_scalar(onehot_n[:, :], idx_row[:, :], const[:, C_PCOL:C_PCOL + 1], None,
                              ALU.is_equal).then_inc(setup, 1)
            dve.wait_ge(setup, 3)
            dve.tensor_tensor(cond_prod, cond_all.unsqueeze(1).to_broadcast([P, groups, T, N]),
                              onehot_slot[:, :, :].unsqueeze(2).to_broadcast([P, groups, T, N]),
                              ALU.mult).then_inc(setup, 1)
            dve.wait_ge(setup, 4)
            dve.tensor_tensor(fbias[0:N], onehot_n[0:N, :].unsqueeze(2).to_broadcast([N, B, T]),
                              fs[:, :].unsqueeze(1).to_broadcast([N, B, T]), ALU.mult).then_inc(fbias_made, 1)
            dve.wait_ge(setup, 5)
            dve.tensor_reduce(cond_sel, cond_prod, AX.X, ALU.add).then_inc(setup, 1)
            dve.wait_ge(setup, 6)
            dve.tensor_tensor(cond_blk, cond_sel.unsqueeze(2).to_broadcast([P, groups, SLOTS, T]),
                              const[:, C_SLOT:C_SLOT + SLOTS].unsqueeze(1).unsqueeze(3)
                              .to_broadcast([P, groups, SLOTS, T]), ALU.mult).then_inc(cond_made, 1)
            dve.tensor_scalar(adapter_mask[:, :], idx_row[:, :], const[:, C_NCOL:C_NCOL + 1], None,
                              ALU.is_equal).then_inc(setup, 1)
            dve.tensor_tensor(k_bias[:, :, :], bias[:, B_K:B_K + DC].unsqueeze(2).to_broadcast([P, DC, 2]),
                              parity.unsqueeze(1).to_broadcast([P, DC, 2]), ALU.mult).then_inc(setup, 1)
            dve.tensor_copy(ident_bf[:, :], const[:, C_ID:C_ID + P]).then_inc(ident_made, 1)
            dve.tensor_copy(causal_bf[:, :, :], const[:, C_CAUSAL:C_CAUSAL + T].unsqueeze(1)
                            .to_broadcast([P, 16, T])).then_inc(causal_made, 1)

            for s in range(HALVES):
                for c in range(DC):
                    dve.wait_ge(xc_hi_made, DC * s + c + 1)
                    free(dve.tensor_tensor(act_lo[:, c, half(s)], tile("xc", s, c)[:, :],
                                           f32(act_hi[:, c, half(s)]), ALU.subtract), "xc", s, c)

            def keys(s):
                dve.wait_ge(setup, 8)
                for m in range(DC):
                    wait_full(dve, "k", s, m)
                    ps = tile("k", s, m)[:, :].rearrange("p (b t) -> p b t", t=T)
                    for e in range(2):
                        last = dve.tensor_scalar(k_x[:, m, s * BH:(s + 1) * BH, e], ps, parity[:, e:e + 1],
                                                 k_bias[:, m, e:e + 1], ALU.mult, ALU.add)
                    free(last, "k", s, m)

            def maxima(s):
                for i in range(PAIRS):
                    n = PAIRS * s + i
                    wait_full(dve, "s", s, i)
                    ps = tile("s", s, i)[:, :].rearrange("p (r k) -> p r k", k=T)
                    dve.tensor_reduce(row_max[:, s, i, :], ps, AX.X, ALU.max).then_inc(max_made, 1)
                    dve.wait_ge(max_made, n + 1)
                    free(dve.tensor_tensor(prob[:, s, i], ps, row_max[:, s, i, :].unsqueeze(2)
                                           .to_broadcast([P, 16, T]), ALU.subtract), "s", s, i)

            def normalise(s):
                for i in range(PAIRS):
                    n = PAIRS * s + i
                    dve.wait_ge(exp_made, n + 1)
                    dve.tensor_reduce(row_sum[:, s, i, :], prob[:, s, i], AX.X, ALU.add).then_inc(sum_made, 1)
                    dve.wait_ge(sum_made, n + 1)
                    dve.reciprocal(row_inv[:, s, i, :], row_sum[:, s, i, :]).then_inc(inv_made, 1)
                    dve.wait_ge(inv_made, n + 1)
                    dve.tensor_tensor(prob[:, s, i], prob[:, s, i], row_inv[:, s, i, :].unsqueeze(2)
                                      .to_broadcast([P, 16, T]), ALU.mult).then_inc(normed, 1)
                    dve.wait_ge(normed, n + 1)
                    dve.transpose(prob_t[:, s, i].rearrange("p r k -> p (r k)"),
                                  prob[:, s, i].rearrange("p r k -> p (r k)")).then_inc(prob_t_made, 1)

            keys(0)
            maxima(0)
            keys(1)
            normalise(0)
            maxima(1)
            normalise(1)

            for s in range(HALVES):
                for j in range(SLOTS):
                    dve.wait_ge(y_even, SLOTS * s + j + 1)
                    ps = tile("y", s, j)[:, :].rearrange("p (h c g t) -> p h c g t", h=2, c=DC, g=GROUPS)
                    for c in range(DC):
                        y = by_slot(s, j)[:, c]
                        last = dve.scalar_tensor_tensor(out=y, in0=ps[:, 1, c], scalar=parity[:, 1:2], in1=y,
                                                        op0=ALU.mult, op1=ALU.add)
                    free(last, "y", s, j)
                for c in range(DC):
                    dve.wait_ge(y_hi_made, DC * s + c + 1)
                    dve.scalar_tensor_tensor(out=aux_lo[:, c, half(s)], in0=q_t[:, c, half(s)],
                                             scalar=bias[:, B_V + c:B_V + c + 1],
                                             in1=f32(aux_hi[:, c, half(s)]), op0=ALU.add,
                                             op1=ALU.subtract).then_inc(y_split, 1)
            dve.wait_ge(resid_loaded, 16)
            for s in range(HALVES):
                for m in range(DC):
                    wait_full(dve, "o", s, m)
                    free(dve.scalar_tensor_tensor(out=resid[:, m, half(s)], in0=tile("o", s, m)[:, :],
                                                  scalar=bias[:, B_O + m:B_O + m + 1],
                                                  in1=resid[:, m, half(s)], op0=ALU.add, op1=ALU.add), "o", s, m)

            def slot_free(n):
                if n >= 4:
                    dve.wait_ge(prod_split, n - 3)

            def mask_adapters(n, name, s, m):
                slot_free(n)
                wait_full(dve, name, s, m)
                free(dve.tensor_tensor(tmp_b[:, n % 4, :].rearrange("p (b t) -> p b t", t=T),
                                       tile(name, s, m)[:, :].rearrange("p (b t) -> p b t", t=T),
                                       adapter_mask[:, s * BH:(s + 1) * BH].unsqueeze(2)
                                       .to_broadcast([P, BH, T]), ALU.mult), name, s, m)

            def gated(n, silus, gate, name, s, m):
                slot_free(n)
                wait_read(dve, gate, s, m)
                wait_full(dve, name, s, m)
                free(dve.tensor_tensor(tmp_b[:, n % 4, :], tile(name, s, m)[:, :], tmp_a[:, silus % 4, :],
                                       ALU.mult), name, s, m)

            dve.wait_ge(w2_split, 4)
            for s in range(HALVES):
                for a in range(2):
                    mask_adapters(Z + 2 * s + a, "z", s, a)
            for m in range(HC):
                for s in range(HALVES):
                    gated(GU + 2 * m + s, 2 * m + s, "gate", "up", s, m)
            for s in range(HALVES):
                mask_adapters(ZD + s, "zd", s, 0)
            for s in range(HALVES):
                for m, name in enumerate(("d0", "d1")):
                    dve.wait_ge(y2_hi_made, DC * s + m + 1)
                    free(dve.tensor_tensor(act_lo[:, m, half(s)], tile(name, s, 0)[:, :],
                                           f32(act_hi[:, m, half(s)]), ALU.subtract), name, s, 0)
            for m in range(HC):
                for s in range(HALVES):
                    gated(FF + 2 * m + s, 2 * HC + 2 * m + s, "f1", "f3", s, m)
            for m in range(DC):
                for s in range(HALVES):
                    n = LAST + m * HALVES + s
                    slot_free(n) if n - 4 < LAST else None
                    wait_full(dve, "w2", s, m)
                    dve.tensor_tensor(tmp_b[:, n % 4, :], tile("w2", s, m)[:, :], resid[:, m, half(s)],
                                      ALU.add).then_inc(out_made, 1)

        @block.gpsimd
        def _(pool):
            def weights_lo(n):
                at = PLACES[n][0]
                pool.wait_ge(w_hi_made, n + 1)
                pool.tensor_tensor(w_lo[:, at:at + COLS[n]], raw[:, n % STAGES, 0:COLS[n]],
                                   f32(w_hi[:, at:at + COLS[n]]), ALU.subtract).then_inc(w_lo_made, 1)

            for n in range(W_A + 1):
                weights_lo(n)
            for j in range(4):
                wait_read(pool, "fold", 0, j)
            for stage in range(3):
                src, dst = (tmp_a, tmp_b) if stage % 2 == 0 else (tmp_b, tmp_a)
                if stage:
                    pool.wait_ge(butterfly, 2 * stage)
                w = D << stage
                a, b = (t[:, :, :].rearrange("p j n -> p (j n)").rearrange("p (u t w) -> p t u w", t=2, w=w)
                        for t in (src, dst))
                pool.tensor_tensor(b[:, 0], a[:, 0], a[:, 1], ALU.add).then_inc(butterfly, 1)
                pool.tensor_tensor(b[:, 1], a[:, 0], a[:, 1], ALU.subtract).then_inc(butterfly, 1)
            weights_lo(W_GU)
            weights_lo(W_GU + 1)
            for j in range(4):
                pool.wait_ge(w2_hi_made, j + 1)
                hi, lo = (t[:, 2 * j:2 * j + 2, :].rearrange("p k d -> p (k d)") for t in (w2_hi, w2_lo))
                pool.tensor_tensor(lo, tmp_b[:, j, :], f32(hi), ALU.subtract).then_inc(w2_split, 1)
            for s in range(HALVES):
                for m in range(DC):
                    pool.wait_ge(x1_hi_made, DC * s + m + 1)
                    pool.tensor_tensor(act_lo[:, m, half(s)], resid[:, m, half(s)],
                                       f32(act_hi[:, m, half(s)]), ALU.subtract).then_inc(x1_split, 1)

            def product_lo(n, hi, lo):
                pool.wait_ge(prod_hi_made, n + 1)
                pool.tensor_tensor(lo, tmp_b[:, n % 4, :], f32(hi), ALU.subtract).then_inc(prod_split, 1)

            for n in range(4):
                product_lo(Z + n, aux_hi[:, n % 2, half(n // 2)], aux_lo[:, n % 2, half(n // 2)])
            weights_lo(W_GU + 2)
            for m in range(HC):
                weights_lo(W_GU + m + 3)
                for s in range(HALVES):
                    product_lo(GU + 2 * m + s, h_hi[:, m, half(s)], h_lo[:, m, half(s)])
            for s in range(HALVES):
                product_lo(ZD + s, aux_hi[:, 0, half(s)], aux_lo[:, 0, half(s)])
            weights_lo(W_GU + HC + 3)
            for m in range(HC):
                weights_lo(W_F + m)
                if m:
                    for s in range(HALVES):
                        product_lo(FF + 2 * m - 2 + s, h_hi[:, m - 1, half(s)], h_lo[:, m - 1, half(s)])
            for s in range(HALVES):
                product_lo(FF + 2 * HC - 2 + s, h_hi[:, HC - 1, half(s)], h_lo[:, HC - 1, half(s)])


def shape_constants():
    p = np.arange(P)
    c = np.zeros((P, C_END), np.float32)
    bits = np.array([[bin(i & j).count("1") for j in p] for i in p])
    c[:, C_HAD:C_HAD + P] = np.where(bits % 2, -1.0, 1.0) / 32.0
    c[:, C_ONES:C_ONES + P] = 1.0
    c[:, C_ID:C_ID + P] = np.eye(P)
    c[:, C_CAUSAL:C_CAUSAL + T] = np.where(np.arange(T)[None, :] > (p % T)[:, None], MASKED, 0.0)
    c[:, C_NROW:C_NROW + N] = np.arange(N)
    c[:, C_NCOL] = p // R
    c[:, C_PCOL] = p
    c[:, C_PAR] = (p // DH) % 2 == 0
    c[:, C_PAR + 1] = (p // DH) % 2 == 1
    c[:, C_SLOT:C_SLOT + SLOTS] = (p // T)[:, None] == np.arange(SLOTS)
    return c


def pack_weights(w_qkv, w_out, wg, wu, wd, ag, bg, au, bu, ad, bd, w1, w3):
    def k(w, m0, m1):
        return [w[c:c + P, m0:m1] for c in range(0, w.shape[0], P)]

    def flat_a(a):
        return a.transpose(1, 0, 2).reshape(a.shape[1], N * R)

    def flat_b(b):
        return b.reshape(N * R, b.shape[2])

    ag, au, ad, bg, bu, bd = flat_a(ag), flat_a(au), flat_a(ad), flat_b(bg), flat_b(bu), flat_b(bd)
    parts = []
    for m in range(2 * DC):
        parts += k(w_qkv, m * P, (m + 1) * P)
    parts += k(w_qkv, 2 * D, 3 * D)
    for m in range(DC):
        parts += k(w_out, m * P, (m + 1) * P)
    parts += k(ag, 0, P) + k(au, 0, P)
    for m in range(0, H, P):
        parts += k(wg, m, m + P) + k(bg, m, m + P) + k(wu, m, m + P) + k(bu, m, m + P)
    parts += k(wd, 0, P) + k(ad, 0, P) + k(wd, P, D) + k(bd, 0, P) + k(bd, P, D)
    for m in range(0, H, P):
        parts += k(w1.T, m, m + P) + k(w3.T, m, m + P)
    return np.ascontiguousarray(np.concatenate(parts, axis=1))


def kernel(x, itok_B_0_7, fside_8xS_0, L0_cond_weights, L0_attn_W_qkv, L0_attn_b_qkv, L0_attn_W_out,
           L0_attn_b_out, L0_cond2_Wg, L0_cond2_Wu, L0_cond2_Wd, L0_cond2_Ag, L0_cond2_Bg, L0_cond2_Au,
           L0_cond2_Bu, L0_cond2_Ad, L0_cond2_Bd, L0_ffn_W1, L0_ffn_W2, L0_ffn_W3):
    import concourse.bacc as bacc
    from concourse.bass_utils import run_bass_kernel_spmd

    x = np.asarray(x)
    arrays = {
        "x_slots": x.reshape(HALVES * GROUPS, P, D).transpose(1, 0, 2),
        "x_feat": x.reshape(TOK, DC, P).transpose(2, 1, 0),
        "index": np.asarray(itok_B_0_7),
        "index_slots": np.asarray(itok_B_0_7).reshape(HALVES * GROUPS, SLOTS).T,
        "fside": np.asarray(fside_8xS_0),
        "cond_w": np.asarray(L0_cond_weights).transpose(1, 2, 0),
        "biases": np.concatenate([np.asarray(L0_attn_b_qkv), np.asarray(L0_attn_b_out)]).reshape(4 * DC, P).T,
        "w_stream": pack_weights(*[np.asarray(a) for a in (
            L0_attn_W_qkv, L0_attn_W_out, L0_cond2_Wg, L0_cond2_Wu, L0_cond2_Wd, L0_cond2_Ag, L0_cond2_Bg,
            L0_cond2_Au, L0_cond2_Bu, L0_cond2_Ad, L0_cond2_Bd, L0_ffn_W1, L0_ffn_W3)]),
        "w2_t": np.asarray(L0_ffn_W2).T.reshape(HC, P, D).transpose(1, 0, 2).reshape(P, HC * D),
        "consts": shape_constants(),
    }
    nc = bacc.Bacc("TRN2", target_bir_lowering=False, num_devices=1)
    args = []
    for name in arrays:
        a = arrays[name] = np.ascontiguousarray(arrays[name])
        args.append(nc.dram_tensor(name, a.shape, mybir.dt.from_np(a.dtype), kind="ExternalInput").ap())
    args.append(nc.dram_tensor("out_feat", (D, TOK), F32, kind="ExternalOutput").ap())
    build(nc, *args)
    r = run_bass_kernel_spmd(nc, [arrays], core_ids=[0])
    return np.ascontiguousarray(r.results[0]["out_feat"].T).reshape(B, T, D)
```

```python
from contextlib import ExitStack

import numpy as np

import concourse.bass as bass
from concourse import mybir

F32 = mybir.dt.float32
F32R = mybir.dt.float32r
BF16 = mybir.dt.bfloat16
I32 = mybir.dt.int32
ALU = mybir.AluOpType
ACT = mybir.ActivationFunctionType
AX = mybir.AxisListType

P = 128
B, T, D = 32, 32, 256
TOK = B * T
HALVES = 2
NG = TOK // P
HT = TOK // HALVES
BH = B // HALVES
SLOTS = P // T
GROUPS = BH // SLOTS
DC = D // P
NH, DH = 16, 16
PAIRS = P // (2 * DH)
QUADS = PAIRS // 2
QR = P // QUADS
TILES_S = DC * QUADS
TILES_Y = DC * SLOTS // 2
N, R = 8, 16
H = 1024
HC = H // P
SCALE = 1.0 / DH
MASKED = -1e30

C_CAUSAL = 0
C_NROW = C_CAUSAL + T
C_NCOL = C_NROW + N
C_PCOL = C_NCOL + 1
C_PAR = C_PCOL + 1
C_FOUR = C_PAR + 2
C_ODD = C_FOUR + 4
C_SLOT = C_ODD + 2
C_COND = C_SLOT + SLOTS
C_FSIDE = C_COND + T * N
C_BIAS = C_FSIDE + T
C_END = C_BIAS + 4 * DC
B_Q, B_K, B_V, B_O = (C_BIAS + i * DC for i in range(4))

W_Q, W_K, W_V, W_OUT, W_A, W_GU = 0, 1, 2, 3, 4, 5
W_D0 = W_GU + HC
W_AD, W_D1, W_BD = W_D0 + 1, W_D0 + 2, W_D0 + 3
W_F = W_BD + 1
BATCHES = W_F + HC
COLS = ([DC * DC * P] * 5 + [(DC + 1) * 2 * P] * HC + [HC * P] * 3 + [DC * P] + [DC * 2 * P] * HC)
RING = 6144
STAGES = 3
STAGE_COLS = max(COLS)
STARTS = [sum(COLS[:i]) for i in range(BATCHES)]


def ring_places():
    places, live, at = [], [], 0
    for n, cols in enumerate(COLS):
        if at + cols > RING:
            at = 0
        need = max([m + 1 for m, lo, hi in live if lo < at + cols and at < hi], default=0)
        live = [(m, lo, hi) for m, lo, hi in live if m + 1 > need] + [(n, at, at + cols)]
        places.append((at, need))
        at += cols
    return places


PLACES = ring_places()
WARM_UP = 12


def psum_tiles():
    names = [("xc", s, c) for s in range(HALVES) for c in range(DC)]

    def qkv(s):
        return [(name, s, m) for m in range(DC) for name in ("q", "k")] + [
            ("v", s, j) for j in range(GROUPS // 2)]

    def scores(s):
        return [("s", s, i) for i in range(TILES_S)]

    names += qkv(0) + [("fold", 0, j) for j in range(4)] + scores(0) + qkv(1) + scores(1)
    names += [("y", s, i) for s in range(HALVES) for i in range(TILES_Y)]
    names += [("o", s, m) for s in range(HALVES) for m in range(DC)]
    names += [("z", s, a) for s in range(HALVES) for a in range(2)]
    names += [(a, s, m) for m in range(HC) for a in ("gate", "up") for s in range(HALVES)]
    names += [(a, s, 0) for a in ("d0", "zd", "d1") for s in range(HALVES)]
    names += [(a, s, m) for m in range(HC) for a in ("f1", "f3") for s in range(HALVES)]
    names += [("w2", s, m) for m in range(DC) for s in range(HALVES)]
    return {name: (n % 8, n // 8) for n, name in enumerate(names)}


TILES = psum_tiles()
LAST_USE = ([("q", 1, 1), ("k", 1, 1), ("v", 1, 1), ("o", 1, 1), ("z", 1, 1)]
            + [("up", 1, m) for m in range(HC)] + [("zd", 1, 0)] * 2 + [("d1", 1, 0)] * 2
            + [("f3", 1, m) for m in range(HC)])
GATED = [(name, s, m) for name in ("up", "f3") for m in range(HC) for s in range(HALVES)]
PRODUCTS = ([("z", s, a) for s in range(HALVES) for a in range(2)] + GATED[:2 * HC]
            + [("zd", s, 0) for s in range(HALVES)] + GATED[2 * HC:])


def build(nc, index, first, x_slots, w_stream, matrices, w2_t, x_feat, out):
    with ExitStack() as ctx:
        def sb(name, shape, dt=F32):
            return ctx.enter_context(nc.sbuf_tensor(name, shape, dt))

        def sem(name):
            return ctx.enter_context(nc.semaphore(name))

        const = sb("const", [P, C_END])
        matrix = sb("matrix", [P, 2 * P])
        index_i = sb("index_i", [P, NG + B], I32)
        index_f = sb("index_f", [P, NG + B])
        had = sb("had", [P, P], F32R)
        ones = sb("ones", [N, P], F32R)
        onehot_slot = sb("onehot_slot", [P, NG, N])
        onehot_n = sb("onehot_n", [P, B])
        adapter_mask = sb("adapter_mask", [P, B])
        fs_hi = sb("fs_hi", [N, T], F32R)
        fs_lo = sb("fs_lo", [N, T])
        cond_sel = sb("cond_sel", [P, NG, T])
        warm = sb("warm", [P, HT], BF16)
        k_bias = sb("k_bias", [P, DC, 4])
        ident_bf = sb("ident_bf", [P, P], BF16)
        causal_bf = sb("causal_bf", [P, 16, T], BF16)
        row_max = sb("row_max", [P, HALVES, TILES_S, 16])
        row_sum = sb("row_sum", [P, HALVES, TILES_S, 16])
        row_inv = sb("row_inv", [P, HALVES, TILES_S, 16])
        resid = sb("resid", [P, DC, TOK])
        raw = sb("raw", [P, STAGES, STAGE_COLS])
        tmp_a = sb("tmp_a", [P, 4, HT])
        tmp_b = sb("tmp_b", [P, 4, HT])
        w_hi = sb("w_hi", [P, RING], F32R)
        w_lo = sb("w_lo", [P, RING], F32R)
        w2_hi = sb("w2_hi", [P, HC, D], F32R)
        w2_lo = sb("w2_lo", [P, HC, D], F32R)
        act_hi = sb("act_hi", [P, DC, TOK], F32R)
        act_lo = sb("act_lo", [P, DC, TOK], F32R)
        aux_hi = sb("aux_hi", [P, DC, TOK], F32R)
        aux_lo = sb("aux_lo", [P, DC, TOK], F32R)
        with ExitStack() as early:
            def eb(name, shape, dt=F32):
                return early.enter_context(nc.sbuf_tensor(name, shape, dt))
            q_t = eb("q_t", [P, DC, TOK])
            k_x = eb("k_x", [P, HALVES, DC, BH, 4, T])
            v_tok = eb("v_tok", [P, NG, D])
            prob = eb("prob", [P, HALVES, TILES_S, 16, T])
        h_hi = sb("h_hi", [P, HC, TOK], F32R)
        h_lo = sb("h_lo", [P, HC, TOK], F32R)
        prob_t = k_x[:, :, :, :, :, :].rearrange("p s c b e t -> p s (c b e t)")\
            .rearrange("p s (i r j q) -> p s i r j q", i=TILES_S, j=2, q=T)
        flat_t = k_x[:, 0].rearrange("p c b e t -> p (c b e t)")
        x_slot = flat_t[:, 0:2048].rearrange("p (g d) -> p g d", d=D)
        cond_prod = flat_t[:, 2048:4096].rearrange("p (g d n) -> p g d n", d=T, n=N)
        cond_all = const[:, C_COND:C_COND + T * N].rearrange("p (d n) -> p d n", n=N)
        fside = const[0:N, C_FSIDE:C_FSIDE + T]
        cond_blk = prob[:, 1, 0:2].rearrange("p i r k -> p (i r k)").rearrange("p (g j d) -> p g j d", j=SLOTS, d=T)
        fb_hi, fb_lo = (w[0:N, RING - TOK:RING].rearrange("p (b d) -> p b d", d=T) for w in (w_hi, w_lo))
        idx_slot = index_f[:, 0:NG]
        idx_row = index_f[:, NG:NG + B]
        parity = const[:, C_PAR:C_PAR + 2]
        slot_of_pair = const[:, C_ODD:C_ODD + 2]
        four = const[:, C_FOUR:C_FOUR + 4]

        banks = [ctx.enter_context(nc.psum_tensor(f"bank{i}", [P, HT], F32)) for i in range(8)]

        index_loaded = sem("index_loaded")
        const_loaded = sem("const_loaded")
        matrix_loaded = sem("matrix_loaded")
        x_loaded = [sem(f"x_loaded{s}") for s in range(HALVES)]
        resid_loaded = sem("resid_loaded")
        w2_loaded = sem("w2_loaded")
        raw_loaded = [sem(f"raw_loaded{j}") for j in range(STAGES)]
        w_hi_made = sem("w_hi_made")
        w_lo_made = sem("w_lo_made")
        bank_full = [sem(f"bank_full{i}") for i in range(8)]
        bank_free = [sem(f"bank_free{i}") for i in range(8)]
        setup = sem("setup")
        ident_made = sem("ident_made")
        causal_made = sem("causal_made")
        had_made = sem("had_made")
        ones_made = sem("ones_made")
        onehot_n_made = sem("onehot_n_made")
        fs_split = sem("fs_split")
        fbias_made = sem("fbias_made")
        warm_made = sem("warm_made")
        z_split = sem("z_split")
        prod_cond = sem("prod_cond")
        sel_made = sem("sel_made")
        blk_made = sem("blk_made")
        adapter_made = sem("adapter_made")
        k_bias_made = sem("k_bias_made")
        w2_raw_hi = sem("w2_raw_hi")
        w2_raw_split = sem("w2_raw_split")
        xc_hi_made = sem("xc_hi_made")
        butterfly = sem("butterfly")
        w2_hi_made = sem("w2_hi_made")
        w2_split = sem("w2_split")
        max_made = sem("max_made")
        exp_made = sem("exp_made")
        sum_made = sem("sum_made")
        inv_made = sem("inv_made")
        normed = sem("normed")
        turned = sem("turned")
        spread = sem("spread")
        prob_t_made = sem("prob_t_made")
        keys_first = sem("keys_first")
        y_even = sem("y_even")
        y_hi_made = sem("y_hi_made")
        y_split = sem("y_split")
        x1_hi_made = sem("x1_hi_made")
        x1_split = sem("x1_split")
        prod_hi_made = sem("prod_hi_made")
        prod_split = sem("prod_split")
        y2_hi_made = sem("y2_hi_made")
        out_made = sem("out_made")
        out_stored = sem("out_stored")

        Z, GU, ZD, FF = 0, 4, 4 + 2 * HC, 6 + 2 * HC
        LAST = FF + 2 * HC

        def tile(name, s, m):
            return banks[TILES[name, s, m][0]]

        def wait_full(eng, name, s, m):
            bank, before = TILES[name, s, m]
            eng.wait_ge(bank_full[bank], before + 1)

        def full(ins, name, s, m):
            ins.then_inc(bank_full[TILES[name, s, m][0]], 1)

        def free(ins, name, s, m):
            ins.then_inc(bank_free[TILES[name, s, m][0]], 1)

        def wait_read(eng, name, s, m):
            bank, before = TILES[name, s, m]
            eng.wait_ge(bank_free[bank], before + 1)

        def half(s):
            return slice(s * HT, (s + 1) * HT)

        def y_cols(s, i):
            return q_t[:, i // 2, half(s)].rearrange("p (g j n) -> p j g n", g=GROUPS, j=SLOTS // 2)[:, i % 2]

        def y_part(s, i, h):
            return tile("y", s, i)[:, h * 2 * P:(h + 1) * 2 * P].rearrange("p (g n) -> p g n", g=GROUPS)

        def f32(ap):
            return ap.bitcast(F32)

        block = ctx.enter_context(nc.Block())

        @block.sync
        def _(sp):
            sp.dma_start(index_i[:, :], index).then_inc(index_loaded, 16)
            sp.dma_start(const[:, :], first).then_inc(const_loaded, 16)

            def load_weights(n):
                if n >= STAGES:
                    sp.wait_ge(w_lo_made, n - STAGES + 1)
                sp.dma_start(raw[:, n % STAGES, 0:COLS[n]], w_stream[:, STARTS[n]:STARTS[n] + COLS[n]])\
                  .then_inc(raw_loaded[n % STAGES], 16)

            for n in range(STAGES):
                load_weights(n)
            sp.dma_start(matrix[:, :], matrices).then_inc(matrix_loaded, 16)
            sp.dma_start(tmp_b[:, :, :], w2_t.rearrange("p (j n) -> p j n", j=4)).then_inc(w2_loaded, 16)
            sp.dma_start(resid[:, :, :], x_feat).then_inc(resid_loaded, 16)
            for n in range(STAGES, BATCHES):
                load_weights(n)
            for j in range(4):
                m, s = j // HALVES, j % HALVES
                sp.wait_ge(out_made, j + 1)
                sp.dma_start(out[m * P:(m + 1) * P, half(s)], tmp_b[:, (LAST + j) % 4, :])\
                  .then_inc(out_stored, 16)
            sp.wait_ge(out_stored, 4 * 16)

        @block.tensor
        def _(pe):
            def claim(name, s, m):
                bank, before = TILES[name, s, m]
                if before:
                    pe.wait_ge(bank_free[bank], before)
                return banks[bank]

            def weights(n):
                pe.wait_ge(w_lo_made, n + 1)
                at = PLACES[n][0]
                return w_hi[:, at:at + COLS[n]], w_lo[:, at:at + COLS[n]]

            def unit(w, u):
                return w[0][:, u * P:(u + 1) * P], w[1][:, u * P:(u + 1) * P]

            def both(tiles, w, xs, start, stop):
                last = []
                for ps, (x_hi, _) in zip(tiles, xs):
                    pe.matmul(ps[:, :], w[0], x_hi, start=start, stop=False)
                for ps, (_, x_lo) in zip(tiles, xs):
                    pe.matmul(ps[:, :], w[0], x_lo, start=False, stop=False)
                for ps, (x_hi, _) in zip(tiles, xs):
                    last.append(pe.matmul(ps[:, :], w[1], x_hi, start=False, stop=stop))
                return last

            def rows(hi, lo, c, ss=(0, 1)):
                return [(hi[:, c, half(s)], lo[:, c, half(s)]) for s in ss]

            pe.wait_ge(warm_made, 1)
            for _ in range(WARM_UP):
                pe.matmul(banks[7][:, :], warm[:, 0:P], warm[:, :], start=True, stop=True)
            for s in range(HALVES):
                for c in range(DC):
                    ps = claim("xc", s, c)
                    if c == 0:
                        pe.wait_ge(blk_made, s + 1)
                        pe.wait_ge(x_loaded[s], 16)
                    for g in range(GROUPS):
                        n = s * GROUPS + g
                        pe.matmul(ps[:, g * P:(g + 1) * P], x_slot[:, n, c * P:(c + 1) * P], cond_blk[:, n],
                                  start=(g == 0), stop=False, skip_group_check=True)
                    if s == 0 and c == 0:
                        pe.wait_ge(ones_made, 1)
                        pe.wait_ge(fbias_made, 2)
                    for fb in (fb_hi, fb_lo):
                        last = pe.matmul(ps[:, :], ones[:, :], fb[:, s * BH:(s + 1) * BH, :], start=False,
                                         stop=fb is fb_lo, skip_group_check=True)
                    full(last, "xc", s, c)

            def qkv(s):
                for c in range(DC):
                    wait_read(pe, "xc", s, c)
                for m in range(DC):
                    for name, n in (("q", W_Q), ("k", W_K)):
                        w = weights(n)
                        ps = claim(name, s, m)
                        for c in range(DC):
                            last = both([ps], unit(w, m * DC + c), rows(act_hi, act_lo, c, [s]),
                                        c == 0, c == DC - 1)
                        full(last[0], name, s, m)
                w = weights(W_V)
                for j in range(GROUPS // 2):
                    ps = claim("v", s, j)
                    for g2 in range(2):
                        for c in range(DC):
                            at = s * HT + (2 * j + g2) * P
                            x_hi, x_lo = act_hi[:, c, at:at + P], act_lo[:, c, at:at + P]
                            wv = [a[:, c * D:(c + 1) * D] for a in w]
                            o = ps[:, g2 * D:(g2 + 1) * D]
                            pe.matmul(o, x_hi, wv[0], start=(c == 0), stop=False)
                            pe.matmul(o, x_hi, wv[1], start=False, stop=False)
                            last = pe.matmul(o, x_lo, wv[0], start=False, stop=(c == DC - 1))
                    full(last, "v", s, j)

            def scores(s):
                pe.wait_ge(ident_made, 1)
                pe.wait_ge(causal_made, 1)
                for c in range(DC):
                    tiles = [claim("s", s, QUADS * c + i) for i in range(QUADS)]
                    for ps in tiles:
                        pe.matmul(ps[:, :], ident_bf[:, :], causal_bf[:, :, :], start=True, stop=False,
                                  skip_group_check=True)
                    wait_read(pe, "q", s, c)
                    wait_read(pe, "k", s, c)
                    for i in range(QUADS):
                        q = slice(QR * i, QR * i + QR)
                        for g in range(GROUPS):
                            for j in range(SLOTS):
                                b = g * SLOTS + j
                                end = g == GROUPS - 1 and j == SLOTS - 1
                                last = pe.matmul(tiles[i][32 * j:32 * j + 32, g * 4 * T:(g + 1) * 4 * T],
                                                 q_t[q, c, (s * BH + b) * T:(s * BH + b + 1) * T],
                                                 k_x[q, s, c, b], start=False, stop=end, skip_group_check=True)
                        full(last, "s", s, QUADS * c + i)

            def fold():
                pe.wait_ge(had_made, 1)
                for j in range(4):
                    ps = claim("fold", 0, j)
                    pe.wait_ge(w2_raw_split, j + 1)
                    pe.matmul(ps[:, :], had[:, :], w2_hi[:, 2 * j:2 * j + 2, :], start=True, stop=False)
                    full(pe.matmul(ps[:, :], had[:, :], w2_lo[:, 2 * j:2 * j + 2, :], start=False, stop=True),
                         "fold", 0, j)

            def values(s):
                for j in range(GROUPS // 2):
                    wait_read(pe, "v", s, j)
                for c in range(DC):
                    tiles = [claim("y", s, 2 * c + i) for i in range(SLOTS // 2)]
                    pe.wait_ge(prob_t_made, TILES_S * s + QUADS * (c + 1))
                    for g in range(GROUPS):
                        for jp in range(SLOTS // 2):
                            rows_ = slice(64 * jp, 64 * jp + 64)
                            for i in range(PAIRS):
                                o = tiles[jp][32 * i:32 * i + 32, :].rearrange(
                                    "p (h g n) -> p g h n", h=2, g=GROUPS)[:, g]
                                at = g * 4 + i % 2 * 2
                                last = pe.matmul(o, v_tok[rows_, s * GROUPS + g, c * P + 32 * i:c * P + 32 * i + 32],
                                                 prob_t[rows_, s, QUADS * c + i // 2, at:at + 2].rearrange(
                                                     "p r j q -> p r (j q)"), start=True, stop=True,
                                                 skip_group_check=True)
                            if g == GROUPS - 1:
                                full(last, "y", s, 2 * c + jp)

            def project(s):
                w = weights(W_OUT)
                for m in range(DC):
                    ps = claim("o", s, m)
                    pe.wait_ge(y_split, DC * (s + 1))
                    for c in range(DC):
                        last = both([ps], unit(w, m * DC + c), rows(aux_hi, aux_lo, c, [s]), c == 0, c == DC - 1)
                    full(last[0], "o", s, m)

            def adapters_in(s):
                w = weights(W_A)
                for a in range(2):
                    ps = claim("z", s, a)
                    pe.wait_ge(x1_split, DC * (s + 1))
                    for c in range(DC):
                        last = both([ps], unit(w, a * DC + c), rows(act_hi, act_lo, c, [s]), c == 0, c == DC - 1)
                    full(last[0], "z", s, a)

            qkv(0)
            fold()
            scores(0)
            qkv(1)
            scores(1)
            values(0)
            values(1)
            project(0)
            project(1)
            adapters_in(0)
            adapters_in(1)

            for m in range(HC):
                w = weights(W_GU + m)
                for a, name in enumerate(("gate", "up")):
                    tiles = [claim(name, s, m) for s in range(HALVES)]
                    for c in range(DC):
                        both(tiles, unit(w, a * (DC + 1) + c), rows(act_hi, act_lo, c), c == 0, False)
                    pe.wait_ge(z_split, 4)
                    last = both(tiles, unit(w, a * (DC + 1) + DC), rows(aux_hi, aux_lo, a), False, True)
                    for s in range(HALVES):
                        full(last[s], name, s, m)

            down = {}
            for name, n in (("d0", W_D0), ("zd", W_AD), ("d1", W_D1)):
                w = weights(n)
                tiles = down[name] = [claim(name, s, 0) for s in range(HALVES)]
                for k in range(HC):
                    pe.wait_ge(prod_split, GU - 4 + 2 * k + 2)
                    last = both(tiles, unit(w, k), rows(h_hi, h_lo, k), k == 0, name == "zd" and k == HC - 1)
                if name == "zd":
                    for s in range(HALVES):
                        full(last[s], name, s, 0)
            w = weights(W_BD)
            pe.wait_ge(prod_split, ZD - 4 + 2)
            for s in range(HALVES):
                for m, name in enumerate(("d0", "d1")):
                    last = both([down[name][s]], unit(w, m), rows(aux_hi, aux_lo, 0, [s]), False, True)
                    full(last[0], name, s, 0)

            for m in range(HC):
                w = weights(W_F + m)
                for a, name in enumerate(("f1", "f3")):
                    tiles = [claim(name, s, m) for s in range(HALVES)]
                    for ss in ([0], [1]) if m == 0 and a == 0 else ([0, 1],):
                        for s in ss:
                            wait_read(pe, "d0", s, 0)
                            wait_read(pe, "d1", s, 0)
                        for c in range(DC):
                            last = both([tiles[s] for s in ss], unit(w, a * DC + c),
                                        rows(act_hi, act_lo, c, ss), c == 0, c == DC - 1)
                        for s, ins in zip(ss, last):
                            full(ins, name, s, m)

            pe.wait_ge(w2_split, 4)
            for m in range(DC):
                tiles = [claim("w2", s, m) for s in range(HALVES)]
                if m == DC - 1:
                    steps = [[0], [1]]
                else:
                    steps = [[0, 1]]
                for ss in steps:
                    for k in range(HC):
                        pe.wait_ge(prod_split, FF - 4 + 2 * k + 2)
                        w = (w2_hi[:, k, m * P:(m + 1) * P], w2_lo[:, k, m * P:(m + 1) * P])
                        last = both([tiles[s] for s in ss], w, rows(h_hi, h_lo, k, ss), k == 0, k == HC - 1)
                    for s, ins in zip(ss, last):
                        full(ins, "w2", s, m)

        @block.scalar
        def _(act):
            for s in range(HALVES):
                act.dma_start(x_slot[:, s * GROUPS:(s + 1) * GROUPS, :],
                              x_slots[:, s * GROUPS:(s + 1) * GROUPS, :]).then_inc(x_loaded[s], 16)

            def split_weights(n):
                act.wait_ge(raw_loaded[n % STAGES], 16 * (n // STAGES + 1))
                at, need = PLACES[n]
                if need:
                    wait_full(act, *LAST_USE[need - 1])
                act.activation(w_hi[:, at:at + COLS[n]], raw[:, n % STAGES, 0:COLS[n]], ACT.Copy)\
                   .then_inc(w_hi_made, 1)

            split_weights(W_Q)
            split_weights(W_K)
            split_weights(W_V)
            for s in range(HALVES):
                for c in range(DC):
                    wait_full(act, "xc", s, c)
                    act.activation(act_hi[:, c, half(s)], tile("xc", s, c)[:, :], ACT.Copy)\
                       .then_inc(xc_hi_made, 1)

            def evacuate_qv(s):
                act.wait_ge(k_bias_made, 1)
                for m in range(DC):
                    wait_full(act, "q", s, m)
                    free(act.activation(q_t[:, m, half(s)], tile("q", s, m)[:, :], ACT.Identity,
                                        bias=const[:, B_Q + m:B_Q + m + 1]), "q", s, m)
                    wait_full(act, "k", s, m)
                    for e in range(2):
                        act.activation(k_x[:, s, m, :, e], tile("k", s, m)[:, :].rearrange(
                            "p (b t) -> p b t", t=T), ACT.Identity, scale=four[:, e:e + 1],
                            bias=k_bias[:, m, e:e + 1]).then_inc(keys_first, 1)
                for j in range(GROUPS // 2):
                    wait_full(act, "v", s, j)
                    g = s * GROUPS + 2 * j
                    free(act.activation(v_tok[:, g:g + 2, :], tile("v", s, j)[:, :].rearrange(
                        "p (g d) -> p g d", g=2), ACT.Copy), "v", s, j)

            def exps(s):
                for i in range(TILES_S):
                    wait_read(act, "s", s, i)
                    act.activation(prob[:, s, i], prob[:, s, i], ACT.Exp, scale=SCALE).then_inc(exp_made, 1)

            def spread_slots(s):
                for i in range(TILES_S):
                    n = TILES_S * s + i
                    act.wait_ge(turned, n + 1)
                    act.activation(prob_t[:, s, i, :, 1], prob_t[:, s, i, :, 0], ACT.Copy,
                                   scale=slot_of_pair[:, 1:2]).then_inc(spread, 1)
                    act.wait_ge(spread, n + 1)
                    act.activation(prob_t[:, s, i, :, 0], prob_t[:, s, i, :, 0], ACT.Copy,
                                   scale=slot_of_pair[:, 0:1]).then_inc(prob_t_made, 1)

            for j in range(4):
                act.wait_ge(w2_loaded, 16)
                act.activation(w2_hi[:, 2 * j:2 * j + 2, :].rearrange("p k d -> p (k d)"), tmp_b[:, j, :],
                               ACT.Copy).then_inc(w2_raw_hi, 1)
            evacuate_qv(0)
            for j in range(4):
                wait_full(act, "fold", 0, j)
                free(act.activation(tmp_a[:, j, :], tile("fold", 0, j)[:, :], ACT.Copy), "fold", 0, j)
            split_weights(W_OUT)
            split_weights(W_A)
            exps(0)
            evacuate_qv(1)
            spread_slots(0)
            exps(1)
            split_weights(W_GU)
            def even_heads(s):
                for i in range(TILES_Y):
                    wait_full(act, "y", s, i)
                    act.activation(y_cols(s, i), y_part(s, i, 0), ACT.Copy, scale=parity[:, 0:1])\
                       .then_inc(y_even, 1)

            def attention_hi(s):
                for c in range(DC):
                    for i in range(2):
                        wait_read(act, "y", s, 2 * c + i)
                    act.activation(aux_hi[:, c, half(s)], q_t[:, c, half(s)], ACT.Identity,
                                   bias=const[:, B_V + c:B_V + c + 1]).then_inc(y_hi_made, 1)

            even_heads(0)
            spread_slots(1)
            split_weights(W_GU + 1)
            attention_hi(0)
            even_heads(1)
            attention_hi(1)
            for j in range(4):
                act.wait_ge(butterfly, 6)
                part = w2_hi[:, 2 * j:2 * j + 2, :].rearrange("p k d -> p (k d)")
                act.activation(part, tmp_b[:, j, :], ACT.Copy).then_inc(w2_hi_made, 1)
            for s in range(HALVES):
                for m in range(DC):
                    wait_read(act, "o", s, m)
                    act.activation(act_hi[:, m, half(s)], resid[:, m, half(s)], ACT.Copy)\
                       .then_inc(x1_hi_made, 1)

            def product_hi(n, dst):
                wait_read(act, *PRODUCTS[n])
                act.activation(dst, tmp_b[:, n % 4, :], ACT.Copy).then_inc(prod_hi_made, 1)

            def silu(n, name, s, m):
                if n == 0:
                    act.wait_ge(butterfly, 6)
                if n >= 4:
                    wait_read(act, *GATED[n - 4])
                wait_full(act, name, s, m)
                free(act.activation(tmp_a[:, n % 4, :], tile(name, s, m)[:, :], ACT.Silu), name, s, m)

            for n in range(4):
                product_hi(Z + n, aux_hi[:, n % 2, half(n // 2)])
            split_weights(W_GU + 2)
            for m in range(HC):
                for s in range(HALVES):
                    silu(2 * m + s, "gate", s, m)
                split_weights(W_GU + m + 3)
                for s in range(HALVES):
                    product_hi(GU + 2 * m + s, h_hi[:, m, half(s)])
            for s in range(HALVES):
                product_hi(ZD + s, aux_hi[:, 0, half(s)])
            split_weights(W_GU + HC + 3)
            split_weights(W_F)
            for s in range(HALVES):
                for m, name in enumerate(("d0", "d1")):
                    wait_full(act, name, s, 0)
                    act.activation(act_hi[:, m, half(s)], tile(name, s, 0)[:, :], ACT.Copy)\
                       .then_inc(y2_hi_made, 1)
            for m in range(HC):
                if m + 1 < HC:
                    split_weights(W_F + m + 1)
                for s in range(HALVES):
                    silu(2 * HC + 2 * m + s, "f1", s, m)
                for s in range(HALVES):
                    product_hi(FF + 2 * m + s, h_hi[:, m, half(s)])

        @block.vector
        def _(dve):
            dve.memset(warm[:, :], 0.0).then_inc(warm_made, 1)
            dve.wait_ge(index_loaded, 16)
            dve.tensor_copy(index_f[:, :], index_i[:, :]).then_inc(setup, 1)
            dve.wait_ge(const_loaded, 16)
            dve.wait_ge(setup, 1)
            dve.tensor_tensor(onehot_slot[:, :, :], idx_slot.unsqueeze(2).to_broadcast([P, NG, N]),
                              const[:, C_NROW:C_NROW + N].unsqueeze(1).to_broadcast([P, NG, N]),
                              ALU.is_equal).then_inc(setup, 1)
            dve.tensor_scalar(onehot_n[:, :], idx_row, const[:, C_PCOL:C_PCOL + 1], None,
                              ALU.is_equal).then_inc(onehot_n_made, 1)
            for s in range(HALVES):
                g = slice(s * GROUPS, (s + 1) * GROUPS)
                dve.wait_ge(setup, 2)
                dve.tensor_tensor(cond_prod[:, g], cond_all.unsqueeze(1).to_broadcast([P, GROUPS, T, N]),
                                  onehot_slot[:, g, :].unsqueeze(2).to_broadcast([P, GROUPS, T, N]),
                                  ALU.mult).then_inc(prod_cond, 1)
                dve.wait_ge(prod_cond, s + 1)
                dve.tensor_reduce(cond_sel[:, g], cond_prod[:, g], AX.X, ALU.add).then_inc(sel_made, 1)
                dve.wait_ge(sel_made, s + 1)
                dve.tensor_tensor(cond_blk[:, g], cond_sel[:, g].unsqueeze(2)
                                  .to_broadcast([P, GROUPS, SLOTS, T]),
                                  const[:, C_SLOT:C_SLOT + SLOTS].unsqueeze(1).unsqueeze(3)
                                  .to_broadcast([P, GROUPS, SLOTS, T]), ALU.mult).then_inc(blk_made, 1)
            dve.tensor_scalar(adapter_mask[:, :], idx_row, const[:, C_NCOL:C_NCOL + 1], None,
                              ALU.is_equal).then_inc(adapter_made, 1)
            dve.tensor_tensor(k_bias[:, :, :], const[:, B_K:B_K + DC].unsqueeze(2).to_broadcast([P, DC, 4]),
                              four.unsqueeze(1).to_broadcast([P, DC, 4]), ALU.mult).then_inc(k_bias_made, 1)
            dve.tensor_copy(causal_bf[:, :, :], const[:, C_CAUSAL:C_CAUSAL + T].unsqueeze(1)
                            .to_broadcast([P, 16, T])).then_inc(causal_made, 1)
            dve.wait_ge(matrix_loaded, 16)
            dve.tensor_copy(had[:, :], matrix[:, 0:P]).then_inc(had_made, 1)
            dve.tensor_copy(ident_bf[:, :], matrix[:, P:2 * P]).then_inc(ident_made, 1)

            for s in range(HALVES):
                for c in range(DC):
                    dve.wait_ge(xc_hi_made, DC * s + c + 1)
                    free(dve.tensor_tensor(act_lo[:, c, half(s)], tile("xc", s, c)[:, :],
                                           f32(act_hi[:, c, half(s)]), ALU.subtract), "xc", s, c)

            def keys(s, m):
                dve.wait_ge(k_bias_made, 1)
                dve.wait_ge(keys_first, 2 * (DC * s + m) + 2)
                ps = tile("k", s, m)[:, :].rearrange("p (b t) -> p b t", t=T)
                for e in range(2, 4):
                    last = dve.tensor_scalar(k_x[:, s, m, :, e], ps, four[:, e:e + 1],
                                             k_bias[:, m, e:e + 1], ALU.mult, ALU.add)
                free(last, "k", s, m)

            def maxima(s):
                for i in range(TILES_S):
                    n = TILES_S * s + i
                    wait_full(dve, "s", s, i)
                    ps = tile("s", s, i)[:, :].rearrange("p (r k) -> p r k", k=T)
                    dve.tensor_reduce(row_max[:, s, i, :], ps, AX.X, ALU.max).then_inc(max_made, 1)
                    dve.wait_ge(max_made, n + 1)
                    free(dve.tensor_tensor(prob[:, s, i], ps, row_max[:, s, i, :].unsqueeze(2)
                                           .to_broadcast([P, 16, T]), ALU.subtract), "s", s, i)

            def normalise(s, c):
                for i in range(QUADS * c, QUADS * (c + 1)):
                    n = TILES_S * s + i
                    dve.wait_ge(exp_made, n + 1)
                    dve.tensor_reduce(row_sum[:, s, i, :], prob[:, s, i], AX.X, ALU.add).then_inc(sum_made, 1)
                    dve.wait_ge(sum_made, n + 1)
                    dve.reciprocal(row_inv[:, s, i, :], row_sum[:, s, i, :]).then_inc(inv_made, 1)

            def turn(s):
                wait_full(dve, "s", s, TILES_S - 1)
                for i in range(TILES_S):
                    dve.wait_ge(normed, TILES_S * s + i + 1)
                    dve.transpose(prob_t[:, s, i, :, 0], prob[:, s, i]).then_inc(turned, 1)

            keys(0, 0)
            keys(0, 1)
            maxima(0)
            normalise(0, 0)
            keys(1, 0)
            normalise(0, 1)
            keys(1, 1)
            turn(0)
            maxima(1)
            normalise(1, 0)
            normalise(1, 1)
            turn(1)

            for s in range(HALVES):
                for i in range(TILES_Y):
                    dve.wait_ge(y_even, TILES_Y * s + i + 1)
                    free(dve.scalar_tensor_tensor(out=y_cols(s, i), in0=y_part(s, i, 1),
                                                  scalar=parity[:, 1:2], in1=y_cols(s, i),
                                                  op0=ALU.mult, op1=ALU.add), "y", s, i)
                for c in range(DC):
                    dve.wait_ge(y_hi_made, DC * s + c + 1)
                    dve.scalar_tensor_tensor(out=aux_lo[:, c, half(s)], in0=q_t[:, c, half(s)],
                                             scalar=const[:, B_V + c:B_V + c + 1],
                                             in1=f32(aux_hi[:, c, half(s)]), op0=ALU.add,
                                             op1=ALU.subtract).then_inc(y_split, 1)
            def first_residual(s):
                for m in range(DC):
                    wait_full(dve, "o", s, m)
                    free(dve.scalar_tensor_tensor(out=resid[:, m, half(s)], in0=tile("o", s, m)[:, :],
                                                  scalar=const[:, B_O + m:B_O + m + 1],
                                                  in1=resid[:, m, half(s)], op0=ALU.add, op1=ALU.add), "o", s, m)
                for m in range(DC):
                    dve.wait_ge(x1_hi_made, DC * s + m + 1)
                    dve.tensor_tensor(act_lo[:, m, half(s)], resid[:, m, half(s)],
                                      f32(act_hi[:, m, half(s)]), ALU.subtract).then_inc(x1_split, 1)

            dve.wait_ge(resid_loaded, 16)
            first_residual(0)
            first_residual(1)

            def slot_free(n):
                if n >= 8:
                    dve.wait_ge(prod_split, n - 7)

            def mask_adapters(n, name, s, m):
                slot_free(n)
                wait_full(dve, name, s, m)
                free(dve.tensor_tensor(tmp_b[:, n % 4, :].rearrange("p (b t) -> p b t", t=T),
                                       tile(name, s, m)[:, :].rearrange("p (b t) -> p b t", t=T),
                                       adapter_mask[:, s * BH:(s + 1) * BH].unsqueeze(2)
                                       .to_broadcast([P, BH, T]), ALU.mult), name, s, m)

            def gated(n, silus, gate, name, s, m):
                slot_free(n)
                wait_read(dve, gate, s, m)
                wait_full(dve, name, s, m)
                free(dve.tensor_tensor(tmp_b[:, n % 4, :], tile(name, s, m)[:, :], tmp_a[:, silus % 4, :],
                                       ALU.mult), name, s, m)

            dve.wait_ge(w2_split, 4)
            dve.wait_ge(adapter_made, 1)
            for s in range(HALVES):
                for a in range(2):
                    mask_adapters(Z + 2 * s + a, "z", s, a)
                for a in range(2):
                    n = Z + 2 * s + a
                    dve.wait_ge(prod_hi_made, n + 1)
                    dve.tensor_tensor(aux_lo[:, a, half(s)], tmp_b[:, n, :], f32(aux_hi[:, a, half(s)]),
                                      ALU.subtract).then_inc(z_split, 1)
            dve.wait_ge(z_split, 4)
            for m in range(HC):
                for s in range(HALVES):
                    gated(GU + 2 * m + s, 2 * m + s, "gate", "up", s, m)
            for s in range(HALVES):
                mask_adapters(ZD + s, "zd", s, 0)
            for s in range(HALVES):
                for m, name in enumerate(("d0", "d1")):
                    dve.wait_ge(y2_hi_made, DC * s + m + 1)
                    free(dve.tensor_tensor(act_lo[:, m, half(s)], tile(name, s, 0)[:, :],
                                           f32(act_hi[:, m, half(s)]), ALU.subtract), name, s, 0)
            for m in range(HC):
                for s in range(HALVES):
                    gated(FF + 2 * m + s, 2 * HC + 2 * m + s, "f1", "f3", s, m)
            for m in range(DC):
                for s in range(HALVES):
                    n = LAST + m * HALVES + s
                    slot_free(n) if n - 4 < LAST else None
                    wait_full(dve, "w2", s, m)
                    dve.tensor_tensor(tmp_b[:, n % 4, :], tile("w2", s, m)[:, :], resid[:, m, half(s)],
                                      ALU.add).then_inc(out_made, 1)

        @block.gpsimd
        def _(pool):
            def weights_lo(n):
                at = PLACES[n][0]
                pool.wait_ge(w_hi_made, n + 1)
                pool.tensor_tensor(w_lo[:, at:at + COLS[n]], raw[:, n % STAGES, 0:COLS[n]],
                                   f32(w_hi[:, at:at + COLS[n]]), ALU.subtract).then_inc(w_lo_made, 1)

            pool.memset(f32(ones[:, :]), 1.0).then_inc(ones_made, 1)
            pool.wait_ge(const_loaded, 16)
            pool.tensor_copy(fs_hi[:, :], fside).then_inc(fs_split, 1)
            pool.wait_ge(fs_split, 1)
            pool.tensor_tensor(fs_lo[:, :], fside, f32(fs_hi[:, :]), ALU.subtract).then_inc(fs_split, 1)

            pool.wait_ge(onehot_n_made, 1)
            for part, fb in ((f32(fs_hi[:, :]), fb_hi), (fs_lo[:, :], fb_lo)):
                if fb is fb_lo:
                    pool.wait_ge(fs_split, 2)
                pool.tensor_tensor(fb, onehot_n[0:N, :].unsqueeze(2).to_broadcast([N, B, T]),
                                   part.unsqueeze(1).to_broadcast([N, B, T]), ALU.mult).then_inc(fbias_made, 1)
            weights_lo(W_Q)
            weights_lo(W_K)
            weights_lo(W_V)
            for j in range(4):
                pool.wait_ge(w2_raw_hi, j + 1)
                hi, lo = (t[:, 2 * j:2 * j + 2, :].rearrange("p k d -> p (k d)") for t in (w2_hi, w2_lo))
                pool.tensor_tensor(lo, tmp_b[:, j, :], f32(hi), ALU.subtract).then_inc(w2_raw_split, 1)
            weights_lo(W_OUT)
            weights_lo(W_A)
            for j in range(4):
                wait_read(pool, "fold", 0, j)

            def butterflies(stage):
                src, dst = (tmp_a, tmp_b) if stage % 2 == 0 else (tmp_b, tmp_a)
                if stage:
                    pool.wait_ge(butterfly, 2 * stage)
                w = D << stage
                a, b = (t[:, :, :].rearrange("p j n -> p (j n)").rearrange("p (u t w) -> p t u w", t=2, w=w)
                        for t in (src, dst))
                pool.tensor_tensor(b[:, 0], a[:, 0], a[:, 1], ALU.add).then_inc(butterfly, 1)
                pool.tensor_tensor(b[:, 1], a[:, 0], a[:, 1], ALU.subtract).then_inc(butterfly, 1)

            def normalised(s):
                for i in range(TILES_S):
                    n = TILES_S * s + i
                    pool.wait_ge(inv_made, n + 1)
                    pool.tensor_tensor(prob[:, s, i], prob[:, s, i], row_inv[:, s, i, :].unsqueeze(2)
                                       .to_broadcast([P, 16, T]), ALU.mult).then_inc(normed, 1)

            butterflies(0)
            normalised(0)
            butterflies(1)
            butterflies(2)
            normalised(1)
            weights_lo(W_GU)
            weights_lo(W_GU + 1)
            for j in range(4):
                pool.wait_ge(w2_hi_made, j + 1)
                hi, lo = (t[:, 2 * j:2 * j + 2, :].rearrange("p k d -> p (k d)") for t in (w2_hi, w2_lo))
                pool.tensor_tensor(lo, tmp_b[:, j, :], f32(hi), ALU.subtract).then_inc(w2_split, 1)

            def product_lo(n, hi, lo):
                pool.wait_ge(prod_hi_made, n + 1)
                pool.tensor_tensor(lo, tmp_b[:, n % 4, :], f32(hi), ALU.subtract).then_inc(prod_split, 1)

            weights_lo(W_GU + 2)
            for m in range(HC):
                weights_lo(W_GU + m + 3)
                for s in range(HALVES):
                    product_lo(GU + 2 * m + s, h_hi[:, m, half(s)], h_lo[:, m, half(s)])
            for s in range(HALVES):
                product_lo(ZD + s, aux_hi[:, 0, half(s)], aux_lo[:, 0, half(s)])
            weights_lo(W_GU + HC + 3)
            for m in range(HC):
                weights_lo(W_F + m)
                if m:
                    for s in range(HALVES):
                        product_lo(FF + 2 * m - 2 + s, h_hi[:, m - 1, half(s)], h_lo[:, m - 1, half(s)])
            for s in range(HALVES):
                product_lo(FF + 2 * HC - 2 + s, h_hi[:, HC - 1, half(s)], h_lo[:, HC - 1, half(s)])


def first_array(cond_w, fside, b_qkv, b_out):
    p = np.arange(P)
    f = np.zeros((P, C_END), np.float32)
    f[:, C_CAUSAL:C_CAUSAL + T] = np.where(np.arange(T)[None, :] > (p % T)[:, None], MASKED, 0.0)
    f[:, C_NROW:C_NROW + N] = np.arange(N)
    f[:, C_NCOL] = p // R
    f[:, C_PCOL] = p
    f[:, C_PAR] = (p // DH) % 2 == 0
    f[:, C_PAR + 1] = (p // DH) % 2 == 1
    f[:, C_FOUR:C_FOUR + 4] = (p // DH)[:, None] % 4 == np.arange(4)
    f[:, C_ODD:C_ODD + 2] = (p // T)[:, None] % 2 == np.arange(2)
    f[:, C_SLOT:C_SLOT + SLOTS] = (p // T)[:, None] == np.arange(SLOTS)
    f[:, C_COND:C_COND + T * N] = np.tile(cond_w.transpose(1, 2, 0).reshape(T, T * N), (SLOTS, 1))
    f[0:N, C_FSIDE:C_FSIDE + T] = fside
    f[:, C_BIAS:] = np.concatenate([b_qkv, b_out]).reshape(4 * DC, P).T
    return f


def shape_matrices():
    p = np.arange(P)
    bits = np.array([[bin(i & j).count("1") for j in p] for i in p])
    return np.concatenate([np.where(bits % 2, -1.0, 1.0) / 32.0, np.eye(P)], axis=1).astype(np.float32)


def pack_weights(w_qkv, w_out, wg, wu, wd, ag, bg, au, bu, ad, bd, w1, w3):
    def k(w, m0, m1):
        return [w[c:c + P, m0:m1] for c in range(0, w.shape[0], P)]

    def flat_a(a):
        return a.transpose(1, 0, 2).reshape(a.shape[1], N * R)

    def flat_b(b):
        return b.reshape(N * R, b.shape[2])

    ag, au, ad, bg, bu, bd = flat_a(ag), flat_a(au), flat_a(ad), flat_b(bg), flat_b(bu), flat_b(bd)
    parts = []
    for m in range(2 * DC):
        parts += k(w_qkv, m * P, (m + 1) * P)
    parts += k(w_qkv, 2 * D, 3 * D)
    for m in range(DC):
        parts += k(w_out, m * P, (m + 1) * P)
    parts += k(ag, 0, P) + k(au, 0, P)
    for m in range(0, H, P):
        parts += k(wg, m, m + P) + k(bg, m, m + P) + k(wu, m, m + P) + k(bu, m, m + P)
    parts += k(wd, 0, P) + k(ad, 0, P) + k(wd, P, D) + k(bd, 0, P) + k(bd, P, D)
    for m in range(0, H, P):
        parts += k(w1.T, m, m + P) + k(w3.T, m, m + P)
    return np.ascontiguousarray(np.concatenate(parts, axis=1))


def kernel(x, itok_B_0_7, fside_8xS_0, L0_cond_weights, L0_attn_W_qkv, L0_attn_b_qkv, L0_attn_W_out,
           L0_attn_b_out, L0_cond2_Wg, L0_cond2_Wu, L0_cond2_Wd, L0_cond2_Ag, L0_cond2_Bg, L0_cond2_Au,
           L0_cond2_Bu, L0_cond2_Ad, L0_cond2_Bd, L0_ffn_W1, L0_ffn_W2, L0_ffn_W3):
    import concourse.bacc as bacc
    from concourse.bass_utils import run_bass_kernel_spmd

    x, index = np.asarray(x), np.asarray(itok_B_0_7)
    arrays = {
        "index": np.concatenate([np.repeat(index.reshape(NG, SLOTS).T, T, axis=0), np.tile(index, (P, 1))],
                                axis=1),
        "first": first_array(*[np.asarray(a) for a in (L0_cond_weights, fside_8xS_0, L0_attn_b_qkv,
                                                       L0_attn_b_out)]),
        "x_slots": x.reshape(NG, P, D).transpose(1, 0, 2),
        "w_stream": pack_weights(*[np.asarray(a) for a in (
            L0_attn_W_qkv, L0_attn_W_out, L0_cond2_Wg, L0_cond2_Wu, L0_cond2_Wd, L0_cond2_Ag, L0_cond2_Bg,
            L0_cond2_Au, L0_cond2_Bu, L0_cond2_Ad, L0_cond2_Bd, L0_ffn_W1, L0_ffn_W3)]),
        "matrices": shape_matrices(),
        "w2_t": np.asarray(L0_ffn_W2).T.reshape(HC, P, D).transpose(1, 0, 2).reshape(P, HC * D),
        "x_feat": x.reshape(TOK, DC, P).transpose(2, 1, 0),
    }
    nc = bacc.Bacc("TRN2", target_bir_lowering=False, num_devices=1)
    args = []
    for name in arrays:
        a = arrays[name] = np.ascontiguousarray(arrays[name])
        args.append(nc.dram_tensor(name, a.shape, mybir.dt.from_np(a.dtype), kind="ExternalInput").ap())
    args.append(nc.dram_tensor("out_feat", (D, TOK), F32, kind="ExternalOutput").ap())
    build(nc, *args)
    r = run_bass_kernel_spmd(nc, [arrays], core_ids=[0])
    return np.ascontiguousarray(r.results[0]["out_feat"].T).reshape(B, T, D)
```

```python
from contextlib import ExitStack

import numpy as np

import concourse.bass as bass
from concourse import mybir

F32 = mybir.dt.float32
F32R = mybir.dt.float32r
BF16 = mybir.dt.bfloat16
I32 = mybir.dt.int32
ALU = mybir.AluOpType
ACT = mybir.ActivationFunctionType
AX = mybir.AxisListType

P = 128
B, T, D = 32, 32, 256
TOK = B * T
HALVES = 2
NG = TOK // P
HT = TOK // HALVES
BH = B // HALVES
SLOTS = P // T
GROUPS = BH // SLOTS
DC = D // P
NH, DH = 16, 16
PAIRS = P // (2 * DH)
QUADS = PAIRS // 2
QR = P // QUADS
TILES_S = DC * QUADS
TILES_Y = DC * SLOTS // 2
N, R = 8, 16
H = 1024
HC = H // P
SCALE = 1.0 / DH
MASKED = -1e30

C_CAUSAL = 0
C_NROW = C_CAUSAL + T
C_NCOL = C_NROW + N
C_PCOL = C_NCOL + 1
C_PAR = C_PCOL + 1
C_FOUR = C_PAR + 2
C_ODD = C_FOUR + 4
C_SLOT = C_ODD + 2
C_COND = C_SLOT + SLOTS
C_FSIDE = C_COND + T * N
C_BIAS = C_FSIDE + T
C_END = C_BIAS + 4 * DC
B_Q, B_K, B_V, B_O = (C_BIAS + i * DC for i in range(4))

W_Q, W_K, W_V, W_OUT, W_A, W_GU = 0, 1, 2, 3, 4, 5
W_D0 = W_GU + HC
W_AD, W_D1, W_BD = W_D0 + 1, W_D0 + 2, W_D0 + 3
W_F = W_BD + 1
BATCHES = W_F + HC
COLS = ([DC * DC * P] * 5 + [(DC + 1) * 2 * P] * HC + [HC * P] * 3 + [DC * P] + [DC * 2 * P] * HC)
RING = 6144
STAGES = 3
STAGE_COLS = max(COLS)
STARTS = [sum(COLS[:i]) for i in range(BATCHES)]


def ring_places():
    places, live, at = [], [], 0
    for n, cols in enumerate(COLS):
        if at + cols > RING:
            at = 0
        need = max([m + 1 for m, lo, hi in live if lo < at + cols and at < hi], default=0)
        live = [(m, lo, hi) for m, lo, hi in live if m + 1 > need] + [(n, at, at + cols)]
        places.append((at, need))
        at += cols
    return places


PLACES = ring_places()
OUTS = [(0, 0, 0, HT), (0, 1, 0, HT), (1, 0, 0, HT), (1, 1, 0, HT // 2), (1, 1, HT // 2, HT)]
WARM_UP = 14
KEEP_WARM = (4, 2, 8, 4)


def psum_tiles():
    names = [("xc", s, c) for s in range(HALVES) for c in range(DC)]

    def qk(s):
        return [(name, s, m) for m in range(DC) for name in ("q", "k")]

    def v(s):
        return [("v", s, j) for j in range(GROUPS // 2)]

    def scores(s):
        return [("s", s, i) for i in range(TILES_S)]

    def values(s, c):
        return [("y", s, 2 * c + i) for i in range(2)]

    names += qk(0) + v(0) + scores(0) + qk(1) + v(1) + scores(1)
    names += values(0, 0) + values(0, 1) + values(1, 0) + values(1, 1) + [("fold", 0, j) for j in range(4)]
    names += [("o", s, m) for s in range(HALVES) for m in range(DC)]
    names += [("z", s, a) for s in range(HALVES) for a in range(2)]
    names += [(a, s, m) for m in range(HC) for a in ("gate", "up") for s in range(HALVES)]
    names += [(a, s, 0) for a in ("d0", "zd", "d1") for s in range(HALVES)]
    names += [(a, s, m) for m in range(HC) for a in ("f1", "f3") for s in range(HALVES)]
    names += [("w2", j, 0) for j in range(len(OUTS))]
    return {name: (n % 8, n // 8) for n, name in enumerate(names)}


TILES = psum_tiles()
LAST_USE = ([("q", 1, 1), ("k", 1, 1), ("v", 1, 1), ("o", 1, 1), ("z", 1, 1)]
            + [("up", 1, m) for m in range(HC)] + [("zd", 1, 0)] * 2 + [("d1", 1, 0)] * 2
            + [("f3", 1, m) for m in range(HC)])
GATED = [(name, s, m) for name in ("up", "f3") for m in range(HC) for s in range(HALVES)]
PRODUCTS = ([("z", s, a) for s in range(HALVES) for a in range(2)] + GATED[:2 * HC]
            + [("zd", s, 0) for s in range(HALVES)] + GATED[2 * HC:])


def build(nc, index, first, x_slots, w_stream, matrices, w2_t, x_feat, out):
    with ExitStack() as ctx:
        def sb(name, shape, dt=F32):
            return ctx.enter_context(nc.sbuf_tensor(name, shape, dt))

        def sem(name):
            return ctx.enter_context(nc.semaphore(name))

        const = sb("const", [P, C_END])
        matrix = sb("matrix", [P, 2 * P])
        index_i = sb("index_i", [P, NG + B], I32)
        index_f = sb("index_f", [P, NG + B])
        had = sb("had", [P, P], F32R)
        ones = sb("ones", [N, P], F32R)
        onehot_slot = sb("onehot_slot", [P, NG, N])
        onehot_n = sb("onehot_n", [P, B])
        adapter_mask = sb("adapter_mask", [P, B])
        fs_hi = sb("fs_hi", [N, T], F32R)
        fs_lo = sb("fs_lo", [N, T])
        cond_sel = sb("cond_sel", [P, NG, T])
        warm = sb("warm", [P, HT], BF16)
        k_bias = sb("k_bias", [P, DC, 4])
        ident_bf = sb("ident_bf", [P, P], BF16)
        causal_bf = sb("causal_bf", [P, 16, T], BF16)
        row_max = sb("row_max", [P, HALVES, TILES_S, 16])
        row_sum = sb("row_sum", [P, HALVES, TILES_S, 16])
        row_inv = sb("row_inv", [P, HALVES, TILES_S, 16])
        resid = sb("resid", [P, DC, TOK])
        raw = sb("raw", [P, STAGES, STAGE_COLS])
        tmp_a = sb("tmp_a", [P, 4, HT])
        tmp_b = sb("tmp_b", [P, 4, HT])
        w_hi = sb("w_hi", [P, RING], F32R)
        w_lo = sb("w_lo", [P, RING], F32R)
        with ExitStack() as folding:
            w2_fold = folding.enter_context(nc.sbuf_tensor("w2_fold", [P, 2, HC * D], F32))
        w2_hi = sb("w2_hi", [P, HC, D], F32R)
        w2_lo = sb("w2_lo", [P, HC, D], F32R)
        act_hi = sb("act_hi", [P, DC, TOK], F32R)
        act_lo = sb("act_lo", [P, DC, TOK], F32R)
        aux_hi = sb("aux_hi", [P, DC, TOK], F32R)
        aux_lo = sb("aux_lo", [P, DC, TOK], F32R)
        with ExitStack() as early:
            def eb(name, shape, dt=F32):
                return early.enter_context(nc.sbuf_tensor(name, shape, dt))
            q_t = eb("q_t", [P, DC, TOK])
            k_x = eb("k_x", [P, HALVES, DC, BH, 4, T])
            v_tok = eb("v_tok", [P, NG, D])
            prob = eb("prob", [P, HALVES, TILES_S, 16, T])
        h_hi = sb("h_hi", [P, HC, TOK], F32R)
        h_lo = sb("h_lo", [P, HC, TOK], F32R)
        prob_t = k_x[:, :, :, :, :, :].rearrange("p s c b e t -> p s (c b e t)")\
            .rearrange("p s (i r j q) -> p s i r j q", i=TILES_S, j=2, q=T)
        flat_t = k_x[:, 0].rearrange("p c b e t -> p (c b e t)")
        x_slot = flat_t[:, 0:2048].rearrange("p (g d) -> p g d", d=D)
        cond_prod = flat_t[:, 2048:4096].rearrange("p (g d n) -> p g d n", d=T, n=N)
        cond_all = const[:, C_COND:C_COND + T * N].rearrange("p (d n) -> p d n", n=N)
        fside = const[0:N, C_FSIDE:C_FSIDE + T]
        cond_blk = prob[:, 1, 0:2].rearrange("p i r k -> p (i r k)").rearrange("p (g j d) -> p g j d", j=SLOTS, d=T)
        fb_hi, fb_lo = (w[0:N, RING - TOK:RING].rearrange("p (b d) -> p b d", d=T) for w in (w_hi, w_lo))
        idx_slot = index_f[:, 0:NG]
        idx_row = index_f[:, NG:NG + B]
        parity = const[:, C_PAR:C_PAR + 2]
        slot_of_pair = const[:, C_ODD:C_ODD + 2]
        four = const[:, C_FOUR:C_FOUR + 4]

        banks = [ctx.enter_context(nc.psum_tensor(f"bank{i}", [P, HT], F32)) for i in range(8)]

        index_loaded = sem("index_loaded")
        const_loaded = sem("const_loaded")
        matrix_loaded = sem("matrix_loaded")
        x_loaded = [sem(f"x_loaded{s}") for s in range(HALVES)]
        resid_loaded = sem("resid_loaded")
        w2_loaded = sem("w2_loaded")
        raw_loaded = [sem(f"raw_loaded{j}") for j in range(STAGES)]
        w_hi_made = sem("w_hi_made")
        w_lo_made = sem("w_lo_made")
        bank_full = [sem(f"bank_full{i}") for i in range(8)]
        bank_free = [sem(f"bank_free{i}") for i in range(8)]
        setup = sem("setup")
        ident_made = sem("ident_made")
        causal_made = sem("causal_made")
        had_made = sem("had_made")
        ones_made = sem("ones_made")
        onehot_n_made = sem("onehot_n_made")
        fs_split = sem("fs_split")
        fbias_made = sem("fbias_made")
        warm_made = sem("warm_made")
        z_split = sem("z_split")
        prod_cond = sem("prod_cond")
        sel_made = sem("sel_made")
        blk_made = sem("blk_made")
        adapter_made = sem("adapter_made")
        k_bias_made = sem("k_bias_made")
        w2_raw_hi = sem("w2_raw_hi")
        w2_raw_split = sem("w2_raw_split")
        xc_hi_made = sem("xc_hi_made")
        butterfly = sem("butterfly")
        w2_hi_made = sem("w2_hi_made")
        w2_split = sem("w2_split")
        max_made = sem("max_made")
        exp_made = sem("exp_made")
        sum_made = sem("sum_made")
        inv_made = sem("inv_made")
        normed = sem("normed")
        turned = sem("turned")
        spread = sem("spread")
        prob_t_made = [[sem(f"prob_t_made{s}{c}") for c in range(DC)] for s in range(HALVES)]
        keys_first = sem("keys_first")
        y_even = sem("y_even")
        y_hi_made = sem("y_hi_made")
        y_split = sem("y_split")
        x1_hi_made = sem("x1_hi_made")
        x1_split = sem("x1_split")
        prod_hi_made = sem("prod_hi_made")
        prod_split = sem("prod_split")
        y2_hi_made = sem("y2_hi_made")
        out_made = sem("out_made")
        out_stored = sem("out_stored")

        Z, GU, ZD, FF = 0, 4, 4 + 2 * HC, 6 + 2 * HC

        def tile(name, s, m):
            return banks[TILES[name, s, m][0]]

        def wait_full(eng, name, s, m):
            bank, before = TILES[name, s, m]
            eng.wait_ge(bank_full[bank], before + 1)

        def full(ins, name, s, m):
            ins.then_inc(bank_full[TILES[name, s, m][0]], 1)

        def free(ins, name, s, m):
            ins.then_inc(bank_free[TILES[name, s, m][0]], 1)

        def wait_read(eng, name, s, m):
            bank, before = TILES[name, s, m]
            eng.wait_ge(bank_free[bank], before + 1)

        def half(s):
            return slice(s * HT, (s + 1) * HT)

        def y_cols(s, i):
            return q_t[:, i // 2, half(s)].rearrange("p (g j n) -> p j g n", g=GROUPS, j=SLOTS // 2)[:, i % 2]

        def y_part(s, i, h):
            return tile("y", s, i)[:, h * 2 * P:(h + 1) * 2 * P].rearrange("p (g n) -> p g n", g=GROUPS)

        def f32(ap):
            return ap.bitcast(F32)

        block = ctx.enter_context(nc.Block())

        @block.sync
        def _(sp):
            sp.dma_start(const[:, :], first).then_inc(const_loaded, 16)

            def load_weights(n):
                if n >= STAGES:
                    sp.wait_ge(w_lo_made, n - STAGES + 1)
                sp.dma_start(raw[:, n % STAGES, 0:COLS[n]], w_stream[:, STARTS[n]:STARTS[n] + COLS[n]])\
                  .then_inc(raw_loaded[n % STAGES], 16)

            for n in range(STAGES):
                load_weights(n)
            sp.dma_start(matrix[:, :], matrices).then_inc(matrix_loaded, 16)
            sp.dma_start(tmp_b[:, :, :], w2_t.rearrange("p (j n) -> p j n", j=4)).then_inc(w2_loaded, 16)
            sp.dma_start(resid[:, :, :], x_feat).then_inc(resid_loaded, 16)
            for n in range(STAGES, BATCHES):
                load_weights(n)
            for j, (m, s, c0, c1) in enumerate(OUTS):
                sp.wait_ge(out_made, j + 1)
                sp.dma_start(out[m * P:(m + 1) * P, s * HT + c0:s * HT + c1], tmp_b[:, min(j, 3), c0:c1])\
                  .then_inc(out_stored, 16)
            sp.wait_ge(out_stored, len(OUTS) * 16)

        @block.tensor
        def _(pe):
            def claim(name, s, m):
                bank, before = TILES[name, s, m]
                if before:
                    pe.wait_ge(bank_free[bank], before)
                return banks[bank]

            def weights(n):
                pe.wait_ge(w_lo_made, n + 1)
                at = PLACES[n][0]
                return w_hi[:, at:at + COLS[n]], w_lo[:, at:at + COLS[n]]

            def unit(w, u):
                return w[0][:, u * P:(u + 1) * P], w[1][:, u * P:(u + 1) * P]

            def both(tiles, w, xs, start, stop):
                last = []
                for ps, (x_hi, _) in zip(tiles, xs):
                    pe.matmul(ps[:, :], w[0], x_hi, start=start, stop=False)
                for ps, (_, x_lo) in zip(tiles, xs):
                    pe.matmul(ps[:, :], w[0], x_lo, start=False, stop=False)
                for ps, (x_hi, _) in zip(tiles, xs):
                    last.append(pe.matmul(ps[:, :], w[1], x_hi, start=False, stop=stop))
                return last

            def rows(hi, lo, c, ss=(0, 1)):
                return [(hi[:, c, half(s)], lo[:, c, half(s)]) for s in ss]

            pe.wait_ge(warm_made, 1)
            for _ in range(WARM_UP):
                pe.matmul(banks[7][:, :], warm[:, 0:P], warm[:, :], start=True, stop=True)
            for s in range(HALVES):
                for c in range(DC):
                    ps = claim("xc", s, c)
                    if c == 0:
                        pe.wait_ge(blk_made, s + 1)
                        pe.wait_ge(x_loaded[s], 16)
                    for g in range(GROUPS):
                        n = s * GROUPS + g
                        pe.matmul(ps[:, g * P:(g + 1) * P], x_slot[:, n, c * P:(c + 1) * P], cond_blk[:, n],
                                  start=(g == 0), stop=False, skip_group_check=True)
                    if s == 0 and c == 0:
                        pe.wait_ge(ones_made, 1)
                        pe.wait_ge(fbias_made, 2)
                    for fb in (fb_hi, fb_lo):
                        last = pe.matmul(ps[:, :], ones[:, :], fb[:, s * BH:(s + 1) * BH, :], start=False,
                                         stop=fb is fb_lo, skip_group_check=True)
                    full(last, "xc", s, c)

            def qk(s):
                for c in range(DC):
                    wait_read(pe, "xc", s, c)
                for m in range(DC):
                    for name, n in (("q", W_Q), ("k", W_K)):
                        w = weights(n)
                        ps = claim(name, s, m)
                        for c in range(DC):
                            last = both([ps], unit(w, m * DC + c), rows(act_hi, act_lo, c, [s]),
                                        c == 0, c == DC - 1)
                        full(last[0], name, s, m)

            def v(s):
                w = weights(W_V)
                for j in range(GROUPS // 2):
                    ps = claim("v", s, j)
                    for g2 in range(2):
                        for c in range(DC):
                            at = s * HT + (2 * j + g2) * P
                            x_hi, x_lo = act_hi[:, c, at:at + P], act_lo[:, c, at:at + P]
                            wv = [a[:, c * D:(c + 1) * D] for a in w]
                            o = ps[:, g2 * D:(g2 + 1) * D]
                            pe.matmul(o, x_hi, wv[0], start=(c == 0), stop=False)
                            pe.matmul(o, x_hi, wv[1], start=False, stop=False)
                            last = pe.matmul(o, x_lo, wv[0], start=False, stop=(c == DC - 1))
                    full(last, "v", s, j)

            def scores(s):
                pe.wait_ge(ident_made, 1)
                pe.wait_ge(causal_made, 1)
                for c in range(DC):
                    tiles = [claim("s", s, QUADS * c + i) for i in range(QUADS)]
                    for ps in tiles:
                        pe.matmul(ps[:, :], ident_bf[:, :], causal_bf[:, :, :], start=True, stop=False,
                                  skip_group_check=True)
                    wait_read(pe, "q", s, c)
                    wait_read(pe, "k", s, c)
                    for i in range(QUADS):
                        q = slice(QR * i, QR * i + QR)
                        for g in range(GROUPS):
                            for j in range(SLOTS):
                                b = g * SLOTS + j
                                end = g == GROUPS - 1 and j == SLOTS - 1
                                last = pe.matmul(tiles[i][32 * j:32 * j + 32, g * 4 * T:(g + 1) * 4 * T],
                                                 q_t[q, c, (s * BH + b) * T:(s * BH + b + 1) * T],
                                                 k_x[q, s, c, b], start=False, stop=end, skip_group_check=True)
                        full(last, "s", s, QUADS * c + i)

            def fold():
                pe.wait_ge(had_made, 1)
                for j in range(4):
                    ps = claim("fold", 0, j)
                    pe.wait_ge(w2_raw_split, j + 1)
                    pe.matmul(ps[:, :], had[:, :], w2_hi[:, 2 * j:2 * j + 2, :], start=True, stop=False)
                    full(pe.matmul(ps[:, :], had[:, :], w2_lo[:, 2 * j:2 * j + 2, :], start=False, stop=True),
                         "fold", 0, j)

            def values(s, c):
                for j in range(GROUPS // 2):
                    wait_read(pe, "v", s, j)
                tiles = [claim("y", s, 2 * c + i) for i in range(SLOTS // 2)]
                for _ in range(KEEP_WARM[2 * s + c]):
                    pe.matmul(tiles[0][:, :], warm[:, 0:P], warm[:, :], start=True, stop=True)
                pe.wait_ge(prob_t_made[s][c], QUADS)
                for g in range(GROUPS):
                    for jp in range(SLOTS // 2):
                        rows_ = slice(64 * jp, 64 * jp + 64)
                        for i in range(PAIRS):
                            o = tiles[jp][32 * i:32 * i + 32, :].rearrange(
                                "p (h g n) -> p g h n", h=2, g=GROUPS)[:, g]
                            at = g * 4 + i % 2 * 2
                            last = pe.matmul(o, v_tok[rows_, s * GROUPS + g, c * P + 32 * i:c * P + 32 * i + 32],
                                             prob_t[rows_, s, QUADS * c + i // 2, at:at + 2].rearrange(
                                                 "p r j q -> p r (j q)"), start=True, stop=True,
                                             skip_group_check=True)
                        if g == GROUPS - 1:
                            full(last, "y", s, 2 * c + jp)

            def project(s):
                w = weights(W_OUT)
                for m in range(DC):
                    ps = claim("o", s, m)
                    pe.wait_ge(y_split, DC * (s + 1))
                    for c in range(DC):
                        last = both([ps], unit(w, m * DC + c), rows(aux_hi, aux_lo, c, [s]), c == 0, c == DC - 1)
                    full(last[0], "o", s, m)

            def adapters_in(s):
                w = weights(W_A)
                for a in range(2):
                    ps = claim("z", s, a)
                    pe.wait_ge(x1_split, DC * (s + 1))
                    for c in range(DC):
                        last = both([ps], unit(w, a * DC + c), rows(act_hi, act_lo, c, [s]), c == 0, c == DC - 1)
                    full(last[0], "z", s, a)

            qk(0)
            v(0)
            scores(0)
            qk(1)
            v(1)
            scores(1)
            values(0, 0)
            values(0, 1)
            values(1, 0)
            values(1, 1)
            fold()
            project(0)
            project(1)
            adapters_in(0)
            adapters_in(1)

            for m in range(HC):
                w = weights(W_GU + m)
                for a, name in enumerate(("gate", "up")):
                    tiles = [claim(name, s, m) for s in range(HALVES)]
                    for c in range(DC):
                        both(tiles, unit(w, a * (DC + 1) + c), rows(act_hi, act_lo, c), c == 0, False)
                    pe.wait_ge(z_split, 4)
                    last = both(tiles, unit(w, a * (DC + 1) + DC), rows(aux_hi, aux_lo, a), False, True)
                    for s in range(HALVES):
                        full(last[s], name, s, m)

            down = {}
            for name, n in (("d0", W_D0), ("zd", W_AD), ("d1", W_D1)):
                w = weights(n)
                tiles = down[name] = [claim(name, s, 0) for s in range(HALVES)]
                for k in range(HC):
                    pe.wait_ge(prod_split, GU - 4 + 2 * k + 2)
                    last = both(tiles, unit(w, k), rows(h_hi, h_lo, k), k == 0, name == "zd" and k == HC - 1)
                if name == "zd":
                    for s in range(HALVES):
                        full(last[s], name, s, 0)
            w = weights(W_BD)
            pe.wait_ge(prod_split, ZD - 4 + 2)
            for s in range(HALVES):
                for m, name in enumerate(("d0", "d1")):
                    last = both([down[name][s]], unit(w, m), rows(aux_hi, aux_lo, 0, [s]), False, True)
                    full(last[0], name, s, 0)

            for m in range(HC):
                w = weights(W_F + m)
                for a, name in enumerate(("f1", "f3")):
                    tiles = [claim(name, s, m) for s in range(HALVES)]
                    for ss in ([0], [1]) if m == 0 and a == 0 else ([0, 1],):
                        for c in range(DC):
                            for s in ss:
                                wait_read(pe, f"d{c}", s, 0)
                            last = both([tiles[s] for s in ss], unit(w, a * DC + c),
                                        rows(act_hi, act_lo, c, ss), c == 0, c == DC - 1)
                        for s, ins in zip(ss, last):
                            full(ins, name, s, m)

            pe.wait_ge(w2_split, 4)
            for js in ([0, 1], [2], [3], [4]):
                tiles = [claim("w2", j, 0) for j in js]
                for k in range(HC):
                    pe.wait_ge(prod_split, FF - 4 + 2 * k + 2)
                    m = OUTS[js[0]][0]
                    w = (w2_hi[:, k, m * P:(m + 1) * P], w2_lo[:, k, m * P:(m + 1) * P])
                    xs = [[h[:, k, s * HT + c0:s * HT + c1] for h in (h_hi, h_lo)]
                          for _, s, c0, c1 in (OUTS[j] for j in js)]
                    outs = [ps[:, c0:c1] for ps, (_, _, c0, c1) in zip(tiles, (OUTS[j] for j in js))]
                    last = both(outs, w, xs, k == 0, k == HC - 1)
                for j, ins in zip(js, last):
                    full(ins, "w2", j, 0)

        @block.scalar
        def _(act):
            act.dma_start(index_i[:, :], index).then_inc(index_loaded, 16)
            for s in range(HALVES):
                act.dma_start(x_slot[:, s * GROUPS:(s + 1) * GROUPS, :],
                              x_slots[:, s * GROUPS:(s + 1) * GROUPS, :]).then_inc(x_loaded[s], 16)

            def split_weights(n):
                act.wait_ge(raw_loaded[n % STAGES], 16 * (n // STAGES + 1))
                at, need = PLACES[n]
                if need:
                    wait_full(act, *LAST_USE[need - 1])
                act.activation(w_hi[:, at:at + COLS[n]], raw[:, n % STAGES, 0:COLS[n]], ACT.Copy)\
                   .then_inc(w_hi_made, 1)

            split_weights(W_Q)
            split_weights(W_K)
            split_weights(W_V)
            for s in range(HALVES):
                for c in range(DC):
                    wait_full(act, "xc", s, c)
                    act.activation(act_hi[:, c, half(s)], tile("xc", s, c)[:, :], ACT.Copy)\
                       .then_inc(xc_hi_made, 1)

            def evacuate_qk(s):
                act.wait_ge(k_bias_made, 1)
                for m in range(DC):
                    wait_full(act, "q", s, m)
                    free(act.activation(q_t[:, m, half(s)], tile("q", s, m)[:, :], ACT.Identity,
                                        bias=const[:, B_Q + m:B_Q + m + 1]), "q", s, m)
                    wait_full(act, "k", s, m)
                    for e in range(2):
                        act.activation(k_x[:, s, m, :, e], tile("k", s, m)[:, :].rearrange(
                            "p (b t) -> p b t", t=T), ACT.Identity, scale=four[:, e:e + 1],
                            bias=k_bias[:, m, e:e + 1]).then_inc(keys_first, 1)

            def evacuate_v(s):
                for j in range(GROUPS // 2):
                    wait_full(act, "v", s, j)
                    g = s * GROUPS + 2 * j
                    free(act.activation(v_tok[:, g:g + 2, :], tile("v", s, j)[:, :].rearrange(
                        "p (g d) -> p g d", g=2), ACT.Copy), "v", s, j)

            def exps(s, *tiles):
                for i in tiles:
                    wait_read(act, "s", s, i)
                    act.activation(prob[:, s, i], prob[:, s, i], ACT.Exp, scale=SCALE).then_inc(exp_made, 1)

            def spread_slots(s, *tiles):
                for i in tiles:
                    n = TILES_S * s + i
                    act.wait_ge(turned, n + 1)
                    act.activation(prob_t[:, s, i, :, 1], prob_t[:, s, i, :, 0], ACT.Copy,
                                   scale=slot_of_pair[:, 1:2]).then_inc(spread, 1)

            for j in range(4):
                act.wait_ge(w2_loaded, 16)
                act.activation(w2_hi[:, 2 * j:2 * j + 2, :].rearrange("p k d -> p (k d)"), tmp_b[:, j, :],
                               ACT.Copy).then_inc(w2_raw_hi, 1)
            evacuate_qk(0)
            evacuate_v(0)
            split_weights(W_OUT)
            split_weights(W_A)
            split_weights(W_GU)
            exps(0, 0, 1, 2, 3)
            evacuate_qk(1)
            spread_slots(0, 0, 1)
            evacuate_v(1)
            split_weights(W_GU + 1)
            spread_slots(0, 2, 3)
            exps(1, 0, 1, 2)

            def even_heads(s, *tiles):
                for i in tiles:
                    wait_full(act, "y", s, i)
                    act.activation(y_cols(s, i), y_part(s, i, 0), ACT.Copy, scale=parity[:, 0:1])\
                       .then_inc(y_even, 1)

            def attention_hi(s):
                for c in range(DC):
                    for i in range(2):
                        wait_read(act, "y", s, 2 * c + i)
                    act.activation(aux_hi[:, c, half(s)], q_t[:, c, half(s)], ACT.Identity,
                                   bias=const[:, B_V + c:B_V + c + 1]).then_inc(y_hi_made, 1)

            spread_slots(1, 0, 1)
            exps(1, 3)
            even_heads(0, 0, 1, 2, 3)
            spread_slots(1, 2, 3)
            attention_hi(0)
            even_heads(1, 0, 1, 2, 3)
            attention_hi(1)
            for j in range(4):
                wait_full(act, "fold", 0, j)
                free(act.activation(w2_fold[:, 0, 2 * j * D:(2 * j + 2) * D],
                                    tile("fold", 0, j)[:, :], ACT.Copy), "fold", 0, j)
            for s in range(HALVES):
                for m in range(DC):
                    wait_read(act, "o", s, m)
                    act.activation(act_hi[:, m, half(s)], resid[:, m, half(s)], ACT.Copy)\
                       .then_inc(x1_hi_made, 1)

            def product_hi(n, dst):
                wait_read(act, *PRODUCTS[n])
                act.activation(dst, tmp_b[:, n % 4, :], ACT.Copy).then_inc(prod_hi_made, 1)

            def silu(n, name, s, m):
                if n >= 4:
                    wait_read(act, *GATED[n - 4])
                wait_full(act, name, s, m)
                free(act.activation(tmp_a[:, n % 4, :], tile(name, s, m)[:, :], ACT.Silu), name, s, m)

            for n in range(4):
                product_hi(Z + n, aux_hi[:, n % 2, half(n // 2)])
            split_weights(W_GU + 2)
            for m in range(HC):
                for s in range(HALVES):
                    silu(2 * m + s, "gate", s, m)
                split_weights(W_GU + m + 3)
                for s in range(HALVES):
                    product_hi(GU + 2 * m + s, h_hi[:, m, half(s)])
            act.wait_ge(butterfly, 6)
            for j in range(4):
                act.activation(w2_hi[:, 2 * j:2 * j + 2, :].rearrange("p k d -> p (k d)"),
                               w2_fold[:, 1, 2 * j * D:(2 * j + 2) * D], ACT.Copy)\
                   .then_inc(w2_hi_made, 1)
            for s in range(HALVES):
                product_hi(ZD + s, aux_hi[:, 0, half(s)])
            split_weights(W_GU + HC + 3)
            split_weights(W_F)
            split_weights(W_F + 1)
            for s in range(HALVES):
                for m, name in enumerate(("d0", "d1")):
                    wait_full(act, name, s, 0)
                    act.activation(act_hi[:, m, half(s)], tile(name, s, 0)[:, :], ACT.Copy)\
                       .then_inc(y2_hi_made, 1)
            for m in range(HC):
                if m + 2 < HC:
                    split_weights(W_F + m + 2)
                for s in range(HALVES):
                    silu(2 * HC + 2 * m + s, "f1", s, m)
                for s in range(HALVES):
                    product_hi(FF + 2 * m + s, h_hi[:, m, half(s)])

        @block.vector
        def _(dve):
            dve.memset(warm[:, :], 0.0).then_inc(warm_made, 1)
            dve.wait_ge(index_loaded, 16)
            dve.tensor_copy(index_f[:, :], index_i[:, :]).then_inc(setup, 1)
            dve.wait_ge(const_loaded, 16)
            dve.wait_ge(setup, 1)
            dve.tensor_tensor(onehot_slot[:, :, :], idx_slot.unsqueeze(2).to_broadcast([P, NG, N]),
                              const[:, C_NROW:C_NROW + N].unsqueeze(1).to_broadcast([P, NG, N]),
                              ALU.is_equal).then_inc(setup, 1)
            dve.tensor_scalar(onehot_n[:, :], idx_row, const[:, C_PCOL:C_PCOL + 1], None,
                              ALU.is_equal).then_inc(onehot_n_made, 1)
            for s in range(HALVES):
                g = slice(s * GROUPS, (s + 1) * GROUPS)
                dve.wait_ge(setup, 2)
                dve.tensor_tensor(cond_prod[:, g], cond_all.unsqueeze(1).to_broadcast([P, GROUPS, T, N]),
                                  onehot_slot[:, g, :].unsqueeze(2).to_broadcast([P, GROUPS, T, N]),
                                  ALU.mult).then_inc(prod_cond, 1)
                dve.wait_ge(prod_cond, s + 1)
                dve.tensor_reduce(cond_sel[:, g], cond_prod[:, g], AX.X, ALU.add).then_inc(sel_made, 1)
                dve.wait_ge(sel_made, s + 1)
                dve.tensor_tensor(cond_blk[:, g], cond_sel[:, g].unsqueeze(2)
                                  .to_broadcast([P, GROUPS, SLOTS, T]),
                                  const[:, C_SLOT:C_SLOT + SLOTS].unsqueeze(1).unsqueeze(3)
                                  .to_broadcast([P, GROUPS, SLOTS, T]), ALU.mult).then_inc(blk_made, 1)
            dve.tensor_scalar(adapter_mask[:, :], idx_row, const[:, C_NCOL:C_NCOL + 1], None,
                              ALU.is_equal).then_inc(adapter_made, 1)
            dve.tensor_tensor(k_bias[:, :, :], const[:, B_K:B_K + DC].unsqueeze(2).to_broadcast([P, DC, 4]),
                              four.unsqueeze(1).to_broadcast([P, DC, 4]), ALU.mult).then_inc(k_bias_made, 1)
            dve.tensor_copy(causal_bf[:, :, :], const[:, C_CAUSAL:C_CAUSAL + T].unsqueeze(1)
                            .to_broadcast([P, 16, T])).then_inc(causal_made, 1)
            dve.wait_ge(matrix_loaded, 16)
            dve.tensor_copy(had[:, :], matrix[:, 0:P]).then_inc(had_made, 1)
            dve.tensor_copy(ident_bf[:, :], matrix[:, P:2 * P]).then_inc(ident_made, 1)

            for s in range(HALVES):
                for c in range(DC):
                    dve.wait_ge(xc_hi_made, DC * s + c + 1)
                    free(dve.tensor_tensor(act_lo[:, c, half(s)], tile("xc", s, c)[:, :],
                                           f32(act_hi[:, c, half(s)]), ALU.subtract), "xc", s, c)

            def keys(s, m):
                dve.wait_ge(k_bias_made, 1)
                dve.wait_ge(keys_first, 2 * (DC * s + m) + 2)
                ps = tile("k", s, m)[:, :].rearrange("p (b t) -> p b t", t=T)
                for e in range(2, 4):
                    last = dve.tensor_scalar(k_x[:, s, m, :, e], ps, four[:, e:e + 1],
                                             k_bias[:, m, e:e + 1], ALU.mult, ALU.add)
                free(last, "k", s, m)

            def maxima(s, *tiles):
                for i in tiles:
                    n = TILES_S * s + i
                    wait_full(dve, "s", s, i)
                    ps = tile("s", s, i)[:, :].rearrange("p (r k) -> p r k", k=T)
                    dve.tensor_reduce(row_max[:, s, i, :], ps, AX.X, ALU.max).then_inc(max_made, 1)
                    dve.wait_ge(max_made, n + 1)
                    free(dve.tensor_tensor(prob[:, s, i], ps, row_max[:, s, i, :].unsqueeze(2)
                                           .to_broadcast([P, 16, T]), ALU.subtract), "s", s, i)

            def sums(s, *tiles):
                for i in tiles:
                    n = TILES_S * s + i
                    dve.wait_ge(exp_made, n + 1)
                    dve.tensor_reduce(row_sum[:, s, i, :], prob[:, s, i], AX.X, ALU.add).then_inc(sum_made, 1)
                    dve.wait_ge(sum_made, n + 1)
                    dve.reciprocal(row_inv[:, s, i, :], row_sum[:, s, i, :]).then_inc(inv_made, 1)

            def turn(s, *tiles):
                wait_full(dve, "s", s, TILES_S - 1)
                for i in tiles:
                    dve.wait_ge(normed, TILES_S * s + i + 1)
                    dve.transpose(prob_t[:, s, i, :, 0], prob[:, s, i]).then_inc(turned, 1)

            keys(0, 0)
            keys(0, 1)
            maxima(0, 0, 1, 2, 3)
            sums(0, 0, 1)
            keys(1, 0)
            turn(0, 0, 1)
            sums(0, 2, 3)
            keys(1, 1)
            turn(0, 2, 3)
            maxima(1, 0, 1)
            sums(1, 0, 1)
            maxima(1, 2)
            turn(1, 0, 1)
            maxima(1, 3)
            sums(1, 2, 3)
            turn(1, 2, 3)
            for i in range(2, 4):
                dve.wait_ge(spread, TILES_S + i + 1)
                dve.tensor_scalar(prob_t[:, 1, i, :, 0], prob_t[:, 1, i, :, 0], slot_of_pair[:, 0:1], None,
                                  ALU.mult).then_inc(prob_t_made[1][1], 1)

            for s in range(HALVES):
                for i in range(TILES_Y):
                    dve.wait_ge(y_even, TILES_Y * s + i + 1)
                    free(dve.scalar_tensor_tensor(out=y_cols(s, i), in0=y_part(s, i, 1),
                                                  scalar=parity[:, 1:2], in1=y_cols(s, i),
                                                  op0=ALU.mult, op1=ALU.add), "y", s, i)
                for c in range(DC):
                    dve.wait_ge(y_hi_made, DC * s + c + 1)
                    dve.scalar_tensor_tensor(out=aux_lo[:, c, half(s)], in0=q_t[:, c, half(s)],
                                             scalar=const[:, B_V + c:B_V + c + 1],
                                             in1=f32(aux_hi[:, c, half(s)]), op0=ALU.add,
                                             op1=ALU.subtract).then_inc(y_split, 1)
            def first_residual(s):
                for m in range(DC):
                    wait_full(dve, "o", s, m)
                    free(dve.scalar_tensor_tensor(out=resid[:, m, half(s)], in0=tile("o", s, m)[:, :],
                                                  scalar=const[:, B_O + m:B_O + m + 1],
                                                  in1=resid[:, m, half(s)], op0=ALU.add, op1=ALU.add), "o", s, m)
                for m in range(DC):
                    dve.wait_ge(x1_hi_made, DC * s + m + 1)
                    dve.tensor_tensor(act_lo[:, m, half(s)], resid[:, m, half(s)],
                                      f32(act_hi[:, m, half(s)]), ALU.subtract).then_inc(x1_split, 1)

            dve.wait_ge(resid_loaded, 16)
            first_residual(0)
            first_residual(1)

            def slot_free(n):
                if n >= 8:
                    dve.wait_ge(prod_split, n - 7)

            def mask_adapters(n, name, s, m):
                slot_free(n)
                wait_full(dve, name, s, m)
                free(dve.tensor_tensor(tmp_b[:, n % 4, :].rearrange("p (b t) -> p b t", t=T),
                                       tile(name, s, m)[:, :].rearrange("p (b t) -> p b t", t=T),
                                       adapter_mask[:, s * BH:(s + 1) * BH].unsqueeze(2)
                                       .to_broadcast([P, BH, T]), ALU.mult), name, s, m)

            def gated(n, silus, gate, name, s, m):
                slot_free(n)
                wait_read(dve, gate, s, m)
                wait_full(dve, name, s, m)
                free(dve.tensor_tensor(tmp_b[:, n % 4, :], tile(name, s, m)[:, :], tmp_a[:, silus % 4, :],
                                       ALU.mult), name, s, m)

            dve.wait_ge(w2_raw_split, 4)
            dve.wait_ge(adapter_made, 1)
            for s in range(HALVES):
                for a in range(2):
                    mask_adapters(Z + 2 * s + a, "z", s, a)
                for a in range(2):
                    n = Z + 2 * s + a
                    dve.wait_ge(prod_hi_made, n + 1)
                    dve.tensor_tensor(aux_lo[:, a, half(s)], tmp_b[:, n, :], f32(aux_hi[:, a, half(s)]),
                                      ALU.subtract).then_inc(z_split, 1)
            dve.wait_ge(z_split, 4)
            for m in range(HC):
                for s in range(HALVES):
                    gated(GU + 2 * m + s, 2 * m + s, "gate", "up", s, m)
            for s in range(HALVES):
                mask_adapters(ZD + s, "zd", s, 0)
            for s in range(HALVES):
                for m, name in enumerate(("d0", "d1")):
                    dve.wait_ge(y2_hi_made, DC * s + m + 1)
                    free(dve.tensor_tensor(act_lo[:, m, half(s)], tile(name, s, 0)[:, :],
                                           f32(act_hi[:, m, half(s)]), ALU.subtract), name, s, 0)
            for m in range(HC):
                for s in range(HALVES):
                    gated(FF + 2 * m + s, 2 * HC + 2 * m + s, "f1", "f3", s, m)
            for j, (m, s, c0, c1) in enumerate(OUTS):
                wait_full(dve, "w2", j, 0)
                dve.tensor_tensor(tmp_b[:, min(j, 3), c0:c1], tile("w2", j, 0)[:, c0:c1],
                                  resid[:, m, s * HT + c0:s * HT + c1], ALU.add).then_inc(out_made, 1)

        @block.gpsimd
        def _(pool):
            def weights_lo(n):
                at = PLACES[n][0]
                pool.wait_ge(w_hi_made, n + 1)
                pool.tensor_tensor(w_lo[:, at:at + COLS[n]], raw[:, n % STAGES, 0:COLS[n]],
                                   f32(w_hi[:, at:at + COLS[n]]), ALU.subtract).then_inc(w_lo_made, 1)

            pool.memset(f32(ones[:, :]), 1.0).then_inc(ones_made, 1)
            pool.wait_ge(const_loaded, 16)
            pool.tensor_copy(fs_hi[:, :], fside).then_inc(fs_split, 1)
            pool.wait_ge(fs_split, 1)
            pool.tensor_tensor(fs_lo[:, :], fside, f32(fs_hi[:, :]), ALU.subtract).then_inc(fs_split, 1)

            pool.wait_ge(onehot_n_made, 1)
            for part, fb in ((f32(fs_hi[:, :]), fb_hi), (fs_lo[:, :], fb_lo)):
                if fb is fb_lo:
                    pool.wait_ge(fs_split, 2)
                pool.tensor_tensor(fb, onehot_n[0:N, :].unsqueeze(2).to_broadcast([N, B, T]),
                                   part.unsqueeze(1).to_broadcast([N, B, T]), ALU.mult).then_inc(fbias_made, 1)
            weights_lo(W_Q)
            weights_lo(W_K)
            weights_lo(W_V)
            for j in range(4):
                pool.wait_ge(w2_raw_hi, j + 1)
                hi, lo = (t[:, 2 * j:2 * j + 2, :].rearrange("p k d -> p (k d)") for t in (w2_hi, w2_lo))
                pool.tensor_tensor(lo, tmp_b[:, j, :], f32(hi), ALU.subtract).then_inc(w2_raw_split, 1)
            weights_lo(W_OUT)
            weights_lo(W_A)
            weights_lo(W_GU)

            def butterflies(stage, t):
                if stage == 0 and t == 0:
                    for j in range(4):
                        wait_read(pool, "fold", 0, j)
                if stage:
                    pool.wait_ge(butterfly, 2 * stage)
                w = D << stage
                a, b = (w2_fold[:, (stage + x) % 2].rearrange("p (u t w) -> p t u w", t=2, w=w) for x in range(2))
                pool.tensor_tensor(b[:, t], a[:, 0], a[:, 1], ALU.subtract if t else ALU.add)\
                    .then_inc(butterfly, 1)

            def normalised(s, *tiles):
                for i in tiles:
                    n = TILES_S * s + i
                    pool.wait_ge(inv_made, n + 1)
                    pool.tensor_tensor(prob[:, s, i], prob[:, s, i], row_inv[:, s, i, :].unsqueeze(2)
                                       .to_broadcast([P, 16, T]), ALU.mult).then_inc(normed, 1)

            def spread_first(s, *tiles):
                for i in tiles:
                    pool.wait_ge(spread, TILES_S * s + i + 1)
                    pool.tensor_tensor(prob_t[:, s, i, :, 0], prob_t[:, s, i, :, 0],
                                       slot_of_pair[:, 0:1].unsqueeze(2).to_broadcast([P, 16, T]),
                                       ALU.mult).then_inc(prob_t_made[s][i // QUADS], 1)

            normalised(0, 0, 1, 2, 3)
            spread_first(0, 0, 1, 2, 3)
            normalised(1, 0, 1)
            spread_first(1, 0, 1)
            normalised(1, 2, 3)
            weights_lo(W_GU + 1)

            def product_lo(n, hi, lo):
                pool.wait_ge(prod_hi_made, n + 1)
                pool.tensor_tensor(lo, tmp_b[:, n % 4, :], f32(hi), ALU.subtract).then_inc(prod_split, 1)

            weights_lo(W_GU + 2)
            for m in range(HC):
                weights_lo(W_GU + m + 3)
                if m < 6:
                    butterflies(m // 2, m % 2)
                for s in range(HALVES):
                    product_lo(GU + 2 * m + s, h_hi[:, m, half(s)], h_lo[:, m, half(s)])
            for j in range(4):
                pool.wait_ge(w2_hi_made, j + 1)
                hi, lo = (t[:, 2 * j:2 * j + 2, :].rearrange("p k d -> p (k d)") for t in (w2_hi, w2_lo))
                pool.tensor_tensor(lo, w2_fold[:, 1, 2 * j * D:(2 * j + 2) * D], f32(hi), ALU.subtract)\
                    .then_inc(w2_split, 1)
            for s in range(HALVES):
                product_lo(ZD + s, aux_hi[:, 0, half(s)], aux_lo[:, 0, half(s)])
            weights_lo(W_GU + HC + 3)
            weights_lo(W_F)
            weights_lo(W_F + 1)
            for m in range(HC):
                if m + 2 < HC:
                    weights_lo(W_F + m + 2)
                for s in range(HALVES):
                    product_lo(FF + 2 * m + s, h_hi[:, m, half(s)], h_lo[:, m, half(s)])


def first_array(cond_w, fside, b_qkv, b_out):
    p = np.arange(P)
    f = np.zeros((P, C_END), np.float32)
    f[:, C_CAUSAL:C_CAUSAL + T] = np.where(np.arange(T)[None, :] > (p % T)[:, None], MASKED, 0.0)
    f[:, C_NROW:C_NROW + N] = np.arange(N)
    f[:, C_NCOL] = p // R
    f[:, C_PCOL] = p
    f[:, C_PAR] = (p // DH) % 2 == 0
    f[:, C_PAR + 1] = (p // DH) % 2 == 1
    f[:, C_FOUR:C_FOUR + 4] = (p // DH)[:, None] % 4 == np.arange(4)
    f[:, C_ODD:C_ODD + 2] = (p // T)[:, None] % 2 == np.arange(2)
    f[:, C_SLOT:C_SLOT + SLOTS] = (p // T)[:, None] == np.arange(SLOTS)
    f[:, C_COND:C_COND + T * N] = np.tile(cond_w.transpose(1, 2, 0).reshape(T, T * N), (SLOTS, 1))
    f[0:N, C_FSIDE:C_FSIDE + T] = fside
    f[:, C_BIAS:] = np.concatenate([b_qkv, b_out]).reshape(4 * DC, P).T
    return f


def shape_matrices():
    p = np.arange(P)
    bits = np.array([[bin(i & j).count("1") for j in p] for i in p])
    return np.concatenate([np.where(bits % 2, -1.0, 1.0) / 32.0, np.eye(P)], axis=1).astype(np.float32)


def pack_weights(w_qkv, w_out, wg, wu, wd, ag, bg, au, bu, ad, bd, w1, w3):
    def k(w, m0, m1):
        return [w[c:c + P, m0:m1] for c in range(0, w.shape[0], P)]

    def flat_a(a):
        return a.transpose(1, 0, 2).reshape(a.shape[1], N * R)

    def flat_b(b):
        return b.reshape(N * R, b.shape[2])

    ag, au, ad, bg, bu, bd = flat_a(ag), flat_a(au), flat_a(ad), flat_b(bg), flat_b(bu), flat_b(bd)
    parts = []
    for m in range(2 * DC):
        parts += k(w_qkv, m * P, (m + 1) * P)
    parts += k(w_qkv, 2 * D, 3 * D)
    for m in range(DC):
        parts += k(w_out, m * P, (m + 1) * P)
    parts += k(ag, 0, P) + k(au, 0, P)
    for m in range(0, H, P):
        parts += k(wg, m, m + P) + k(bg, m, m + P) + k(wu, m, m + P) + k(bu, m, m + P)
    parts += k(wd, 0, P) + k(ad, 0, P) + k(wd, P, D) + k(bd, 0, P) + k(bd, P, D)
    for m in range(0, H, P):
        parts += k(w1.T, m, m + P) + k(w3.T, m, m + P)
    return np.ascontiguousarray(np.concatenate(parts, axis=1))


def kernel(x, itok_B_0_7, fside_8xS_0, L0_cond_weights, L0_attn_W_qkv, L0_attn_b_qkv, L0_attn_W_out,
           L0_attn_b_out, L0_cond2_Wg, L0_cond2_Wu, L0_cond2_Wd, L0_cond2_Ag, L0_cond2_Bg, L0_cond2_Au,
           L0_cond2_Bu, L0_cond2_Ad, L0_cond2_Bd, L0_ffn_W1, L0_ffn_W2, L0_ffn_W3):
    import concourse.bacc as bacc
    from concourse.bass_utils import run_bass_kernel_spmd

    x, index = np.asarray(x), np.asarray(itok_B_0_7)
    arrays = {
        "index": np.concatenate([np.repeat(index.reshape(NG, SLOTS).T, T, axis=0), np.tile(index, (P, 1))],
                                axis=1),
        "first": first_array(*[np.asarray(a) for a in (L0_cond_weights, fside_8xS_0, L0_attn_b_qkv,
                                                       L0_attn_b_out)]),
        "x_slots": x.reshape(NG, P, D).transpose(1, 0, 2),
        "w_stream": pack_weights(*[np.asarray(a) for a in (
            L0_attn_W_qkv, L0_attn_W_out, L0_cond2_Wg, L0_cond2_Wu, L0_cond2_Wd, L0_cond2_Ag, L0_cond2_Bg,
            L0_cond2_Au, L0_cond2_Bu, L0_cond2_Ad, L0_cond2_Bd, L0_ffn_W1, L0_ffn_W3)]),
        "matrices": shape_matrices(),
        "w2_t": np.asarray(L0_ffn_W2).T.reshape(HC, P, D).transpose(1, 0, 2).reshape(P, HC * D),
        "x_feat": x.reshape(TOK, DC, P).transpose(2, 1, 0),
    }
    nc = bacc.Bacc("TRN2", target_bir_lowering=False, num_devices=1)
    args = []
    for name in arrays:
        a = arrays[name] = np.ascontiguousarray(arrays[name])
        args.append(nc.dram_tensor(name, a.shape, mybir.dt.from_np(a.dtype), kind="ExternalInput").ap())
    args.append(nc.dram_tensor("out_feat", (D, TOK), F32, kind="ExternalOutput").ap())
    build(nc, *args)
    r = run_bass_kernel_spmd(nc, [arrays], core_ids=[0])
    return np.ascontiguousarray(r.results[0]["out_feat"].T).reshape(B, T, D)
```
